# Optimizing a Trainium2 kernel written in Bass

```python
import numpy as np
import jax
import jax.numpy as jnp

def _softmax(x, axis=-1):
    return jax.nn.softmax(x, axis=axis)

def _gelu(x):
    return jax.nn.gelu(x, approximate=True)

def _silu(x):
    return jax.nn.silu(x)

def _sigmoid(x):
    return jax.nn.sigmoid(x)

def _layernorm(x, axis=-1, eps=1e-05):
    m = jnp.mean(x, axis=axis, keepdims=True)
    v = jnp.var(x, axis=axis, keepdims=True)
    return (x - m) / jnp.sqrt(v + eps)

def _scatter_add(tgt, idx, src, axis=0):
    return tgt.at[idx].add(src)

def _segment_sum(src, seg, n):
    return jax.ops.segment_sum(src, seg, n)
kernel_name = 'mk_flamingo_gated_d1_seqx_r8_c1f298'

def setup_inputs(seed: int=0):
    np.random.seed(seed)
    _w = jnp.asarray

    def _rec_inputs():
        import jax
        import jax.numpy as jnp
        _rk = jax.random.key(seed)
        x = 7.22e-05 + 1 * jax.random.normal(jax.random.fold_in(_rk, 1), (32, 64, 256), jnp.float32)
        _lenS = 64 - jax.random.randint(jax.random.fold_in(_rk, 7), (32,), 0, max(1, 64 // 4) + 1, jnp.int32)
        _lenS2 = 64 - jax.random.randint(jax.random.fold_in(_rk, 8), (32,), 0, max(1, 64 // 4) + 1, jnp.int32)
        _ctx_2048P = jax.random.normal(jax.random.fold_in(_rk, 11), (32, 16, 256), jnp.float32)
        _ctx_2048c = jax.random.dirichlet(jax.random.fold_in(_rk, 511), 0.3 * jnp.ones((16,), jnp.float32), (32, 64))
        _ctx_2048t = jnp.einsum('bsk,bkd->bsd', _ctx_2048c, _ctx_2048P)
        _ctx_2048t = _ctx_2048t * jax.lax.rsqrt(jnp.mean(jnp.square(_ctx_2048t)) + 1e-12) * 0.953939
        ctx_2048 = -0.000514642 + 1.00011 * (_ctx_2048t + 0.3 * jax.random.normal(jax.random.fold_in(_rk, 611), (32, 64, 256), jnp.float32))
        _g = jax.random.normal(jax.random.fold_in(_rk, 9001), (2, 1), jnp.float32)
        _g = jnp.sign(_g) * jnp.maximum(jnp.abs(_g), 1.0) + (_g == 0) * 1.0
        g_xattn = _g[0]
        g_ffn = _g[1]
        return (x, ctx_2048, g_xattn, g_ffn)
    x, ctx_2048, g_xattn, g_ffn = _rec_inputs()

    def _L0_xattn_setup():
        import jax, jax.numpy as jnp
        import numpy as np
        D_MODEL = 256
        NUM_HEADS = 16
        HEAD_DIM = D_MODEL // NUM_HEADS

        def _fq_sym(x, axis):
            s = jnp.max(jnp.abs(x), axis=axis, keepdims=True) / 127.0
            s = jnp.maximum(s, 1e-08)
            q = jnp.clip(jnp.round(x / s), -127.0, 127.0) * s
            return x + jax.lax.stop_gradient(q - x)

        def _fq_unsigned(x, axis):
            s = jnp.max(x, axis=axis, keepdims=True) / 255.0
            s = jnp.maximum(s, 1e-08)
            q = jnp.clip(jnp.round(x / s), 0.0, 255.0) * s
            return x + jax.lax.stop_gradient(q - x)
        key = jax.random.key(seed)
        ks = jax.random.split(key, 8)
        B, N, M, C = (2, 256, 64, D_MODEL)
        return {'x': jax.random.normal(ks[0], (B, N, C), jnp.float32), 'cond': jax.random.normal(ks[1], (B, M, C), jnp.float32), 'Wq': jax.random.normal(ks[2], (C, C), jnp.float32) * 0.02, 'bq': jnp.zeros((C,), jnp.float32), 'Wkv': jax.random.normal(ks[3], (C, 2 * C), jnp.float32) * 0.02, 'bkv': jnp.zeros((2 * C,), jnp.float32), 'Wp': jax.random.normal(ks[4], (C, C), jnp.float32) * 0.02, 'bp': jnp.zeros((C,), jnp.float32)}
    _L0_xattn_all = _L0_xattn_setup()
    _L0_xattn_in = {k: v for k, v in _L0_xattn_all.items() if k in ('Wq', 'bq', 'Wkv', 'bkv', 'Wp', 'bp')}
    del _L0_xattn_all

    def _L0_ffn_setup():
        import jax, jax.numpy as jnp
        import numpy as np
        E = 8
        TOP_K = 2
        H = 256
        I_MOE = 176
        I_SH = 704
        B, S = (2, 256)

        def _moe_forward(hidden_states, router_weight, gate_up_proj, down_proj, sh_gate_w, sh_up_w, sh_down_w, shared_gate_w):
            b, s, h = hidden_states.shape
            x = hidden_states.reshape(-1, h)
            shared = jnp.einsum('ti,hi->th', jax.nn.silu(x @ sh_gate_w.T) * (x @ sh_up_w.T), sh_down_w)
            logits = x @ router_weight.T
            probs = jax.nn.softmax(logits.astype(jnp.float32), axis=-1)
            top_v, top_i = jax.lax.top_k(probs, TOP_K)
            top_v = top_v / top_v.sum(axis=-1, keepdims=True)
            combine = (jax.nn.one_hot(top_i, E, dtype=top_v.dtype) * top_v[..., None]).sum(axis=1)
            out = jnp.zeros_like(x)
            for e in range(E):
                gu = x @ gate_up_proj[e].T
                gate, up = (gu[:, :I_MOE], gu[:, I_MOE:])
                cur = jax.nn.silu(gate) * up @ down_proj[e].T
                out = out + cur * combine[:, e:e + 1]
            out = out + jax.nn.sigmoid(x @ shared_gate_w.T) * shared
            return out.reshape(b, s, h)
        key = jax.random.key(seed)
        ks = jax.random.split(key, 8)
        scale = 0.02
        return {'hidden_states': jax.random.normal(ks[0], (B, S, H), dtype=jnp.float32), 'router_weight': jax.random.normal(ks[1], (E, H), dtype=jnp.float32) * scale, 'gate_up_proj': jax.random.normal(ks[2], (E, 2 * I_MOE, H), dtype=jnp.float32) * scale, 'down_proj': jax.random.normal(ks[3], (E, H, I_MOE), dtype=jnp.float32) * scale, 'sh_gate_w': jax.random.normal(ks[4], (I_SH, H), dtype=jnp.float32) * scale, 'sh_up_w': jax.random.normal(ks[5], (I_SH, H), dtype=jnp.float32) * scale, 'sh_down_w': jax.random.normal(ks[6], (H, I_SH), dtype=jnp.float32) * scale, 'shared_gate_w': jax.random.normal(ks[7], (1, H), dtype=jnp.float32) * scale}
    _L0_ffn_all = _L0_ffn_setup()
    _L0_ffn_in = {k: v for k, v in _L0_ffn_all.items() if k in ('router_weight', 'gate_up_proj', 'down_proj', 'sh_gate_w', 'sh_up_w', 'sh_down_w', 'shared_gate_w')}
    del _L0_ffn_all
    return {'x': x, 'ctx_2048': ctx_2048, 'g_xattn': g_xattn, 'g_ffn': g_ffn, 'L0_xattn_Wq': _L0_xattn_in['Wq'], 'L0_xattn_bq': _L0_xattn_in['bq'], 'L0_xattn_Wkv': _L0_xattn_in['Wkv'], 'L0_xattn_bkv': _L0_xattn_in['bkv'], 'L0_xattn_Wp': _L0_xattn_in['Wp'], 'L0_xattn_bp': _L0_xattn_in['bp'], 'L0_ffn_router_weight': _L0_ffn_in['router_weight'], 'L0_ffn_gate_up_proj': _L0_ffn_in['gate_up_proj'], 'L0_ffn_down_proj': _L0_ffn_in['down_proj'], 'L0_ffn_sh_gate_w': _L0_ffn_in['sh_gate_w'], 'L0_ffn_sh_up_w': _L0_ffn_in['sh_up_w'], 'L0_ffn_sh_down_w': _L0_ffn_in['sh_down_w'], 'L0_ffn_shared_gate_w': _L0_ffn_in['shared_gate_w']}

def reference(x, ctx_2048, g_xattn, g_ffn, L0_xattn_Wq, L0_xattn_bq, L0_xattn_Wkv, L0_xattn_bkv, L0_xattn_Wp, L0_xattn_bp, L0_ffn_router_weight, L0_ffn_gate_up_proj, L0_ffn_down_proj, L0_ffn_sh_gate_w, L0_ffn_sh_up_w, L0_ffn_sh_down_w, L0_ffn_shared_gate_w):
    import jax
    import jax.numpy as jnp

    def _L0_xattn_ref(x, cond, Wq, bq, Wkv, bkv, Wp, bp):
        import jax, jax.numpy as jnp
        import numpy as np
        D_MODEL = 256
        NUM_HEADS = 16
        HEAD_DIM = D_MODEL // NUM_HEADS

        def _fq_sym(x, axis):
            s = jnp.max(jnp.abs(x), axis=axis, keepdims=True) / 127.0
            s = jnp.maximum(s, 1e-08)
            q = jnp.clip(jnp.round(x / s), -127.0, 127.0) * s
            return x + jax.lax.stop_gradient(q - x)

        def _fq_unsigned(x, axis):
            s = jnp.max(x, axis=axis, keepdims=True) / 255.0
            s = jnp.maximum(s, 1e-08)
            q = jnp.clip(jnp.round(x / s), 0.0, 255.0) * s
            return x + jax.lax.stop_gradient(q - x)
        B, N, C = x.shape
        H, hd = (NUM_HEADS, HEAD_DIM)
        q = (x @ Wq + bq).reshape(1, B * N, H, hd)
        kv = (cond @ Wkv + bkv).reshape(1, -1, 2, H, hd)
        k, v = (kv[:, :, 0], kv[:, :, 1])
        scale = 1.0 / np.sqrt(hd).astype(np.float32)
        q = jnp.transpose(q * scale, (0, 2, 1, 3))
        k = jnp.transpose(k, (0, 2, 1, 3))
        v = jnp.transpose(v, (0, 2, 1, 3))
        q = _fq_sym(q, axis=-1)
        k = _fq_sym(k, axis=-1)
        v = _fq_sym(v, axis=2)
        attn = jnp.einsum('bhqd,bhkd->bhqk', q, k)
        attn = jax.nn.softmax(attn.astype(jnp.float32), axis=-1)
        attn = _fq_unsigned(attn, axis=-1)
        out = jnp.einsum('bhqk,bhkd->bhqd', attn, v)
        out = jnp.transpose(out, (0, 2, 1, 3)).reshape(B, N, C)
        return out @ Wp + bp

    def _L0_ffn_ref(hidden_states, router_weight, gate_up_proj, down_proj, sh_gate_w, sh_up_w, sh_down_w, shared_gate_w):
        import jax, jax.numpy as jnp
        import numpy as np
        E = 8
        TOP_K = 2
        H = 256
        I_MOE = 176
        I_SH = 704
        B, S = (2, 256)

        def _moe_forward(hidden_states, router_weight, gate_up_proj, down_proj, sh_gate_w, sh_up_w, sh_down_w, shared_gate_w):
            b, s, h = hidden_states.shape
            x = hidden_states.reshape(-1, h)
            shared = jnp.einsum('ti,hi->th', jax.nn.silu(x @ sh_gate_w.T) * (x @ sh_up_w.T), sh_down_w)
            logits = x @ router_weight.T
            probs = jax.nn.softmax(logits.astype(jnp.float32), axis=-1)
            top_v, top_i = jax.lax.top_k(probs, TOP_K)
            top_v = top_v / top_v.sum(axis=-1, keepdims=True)
            combine = (jax.nn.one_hot(top_i, E, dtype=top_v.dtype) * top_v[..., None]).sum(axis=1)
            out = jnp.zeros_like(x)
            for e in range(E):
                gu = x @ gate_up_proj[e].T
                gate, up = (gu[:, :I_MOE], gu[:, I_MOE:])
                cur = jax.nn.silu(gate) * up @ down_proj[e].T
                out = out + cur * combine[:, e:e + 1]
            out = out + jax.nn.sigmoid(x @ shared_gate_w.T) * shared
            return out.reshape(b, s, h)
        return _moe_forward(hidden_states, router_weight, gate_up_proj, down_proj, sh_gate_w, sh_up_w, sh_down_w, shared_gate_w)
    x = x + jnp.tanh(g_xattn[0]) * _L0_xattn_ref(_layernorm(x, axis=-1), ctx_2048, L0_xattn_Wq, L0_xattn_bq, L0_xattn_Wkv, L0_xattn_bkv, L0_xattn_Wp, L0_xattn_bp)
    x = x + jnp.tanh(g_ffn[0]) * _L0_ffn_ref(_layernorm(x, axis=-1), L0_ffn_router_weight, L0_ffn_gate_up_proj, L0_ffn_down_proj, L0_ffn_sh_gate_w, L0_ffn_sh_up_w, L0_ffn_sh_down_w, L0_ffn_shared_gate_w)
    return x

_drawn_inputs = setup_inputs


def setup_inputs(seed=0):
    import zlib

    import numpy as np

    out = dict(_drawn_inputs(seed))
    spreads = {'L0_xattn_bq': (0.0, 0.8), 'L0_xattn_bkv': (0.0, 0.316), 'L0_xattn_bp': (0.0, 0.1)}
    factors = {'ctx_2048': 7.561,
     'L0_xattn_Wq': 8.0,
     'L0_xattn_Wkv': 8.0,
     'L0_ffn_router_weight': 6.964,
     'L0_ffn_gate_up_proj': 6.019,
     'L0_ffn_down_proj': 6.037,
     'L0_ffn_sh_gate_w': 4.275,
     'L0_ffn_sh_up_w': 4.218,
     'L0_ffn_sh_down_w': 4.237,
     'L0_ffn_shared_gate_w': 8.0}
    for name, (base, spread) in spreads.items():
        noise = np.random.default_rng([zlib.crc32(name.encode()), seed]).standard_normal(out[name].shape)
        drawn = base * np.exp(spread * noise) if base else spread * noise
        out[name] = jnp.asarray(drawn.astype(out[name].dtype))
    for name, factor in factors.items():
        out[name] = (out[name] * factor).astype(out[name].dtype)
    return out
```

```python
import concourse.bass as bass
from concourse import mybir
from contextlib import ExitStack
import math

F32 = mybir.dt.float32
BF16 = mybir.dt.bfloat16
F16 = mybir.dt.float16
U16 = mybir.dt.uint16
U8 = mybir.dt.uint8
U32 = mybir.dt.uint32
ALU = mybir.AluOpType
ACT = mybir.ActivationFunctionType
AX = mybir.AxisListType

P = 128
TOKENS = 2048
TILES = TOKENS // P
C = 256
CH = C // P
HEADS = 16
HD = C // HEADS
PAIRS = HEADS // 2
HALF = TOKENS // 2
KT = TOKENS // P
KTH = KT // 2
EXPERTS = 8
I_MOE = 176
I_SH = 704
FEATS = EXPERTS * I_MOE + I_SH
CHUNK = 2 * I_MOE
CHUNKS = FEATS // CHUNK
BLOCKS = -(-FEATS // P)
LAST_BLOCK = FEATS - (BLOCKS - 1) * P
GROUPS = [(g, min(g + 4, BLOCKS)) for g in range(0, BLOCKS, 4)]
ROUND = 1.5 * 2.0 ** 23
MARK = 0x6400
LN_EPS = 1e-5
Q_SCALE = 1.0 / math.sqrt(HD)
LN255 = math.log(255.0)

DVE_A, POOL_A = 6, 5
DVE_FRONT = 12


def build(nc, x, ctx_in, g_xattn, g_ffn, w_q, b_q, w_kv, b_kv, b_v_cols, w_p, b_p, w_route, w_gate, w_up, w_down, out):
    stack = ExitStack()
    with stack:
        def sb(name, shape, dt):
            return stack.enter_context(nc.sbuf_tensor(name, shape, dt))

        def pb(name, shape, dt=F32):
            return stack.enter_context(nc.psum_tensor(name, shape, dt))

        def sem(name):
            return stack.enter_context(nc.semaphore(name))

        x_all = sb("x_all", [P, TILES, C], F32)
        k_cols = sb("k_cols", [P, PAIRS, TOKENS], BF16)
        q_cols = sb("q_cols", [P, HEADS, TOKENS], BF16)
        v_rows = sb("v_rows", [P, KT, C], BF16)
        o_all = sb("o_all", [P, TILES, C], F32)
        s_all = sb("s_all", [P, TILES, 2 * HEADS], F32)
        nsq_all = sb("nsq_all", [P, TILES, HEADS], F32)
        acc_all = sb("acc_all", [P, TILES, 2 * HEADS], F32)
        comb_all = sb("comb_all", [P, TILES, EXPERTS + 1], F32)
        gu_w = sb("gu_w", [P, CH, 2, FEATS], F32)
        d_w = k_cols[:, :, :].rearrange("p j n -> p (j n)").bitcast(F32)[:, 0:BLOCKS * C].rearrange(
            "p (b n) -> p b n", b=BLOCKS)

        w_qk = sb("w_qk", [P, CH, 2 * C], F32)
        w_v = sb("w_v", [P, CH, C], F32)
        w_o = sb("w_o", [P, CH, C], F32)
        w_r = sb("w_r", [P, CH, EXPERTS + 1], F32)
        b_qk = sb("b_qk", [P, 2 * C], F32)
        b_v = sb("b_v", [P, CH], F32)
        b_o = sb("b_o", [P, C], F32)
        gates = sb("gates", [P, 2], F32)
        tgates = sb("tgates", [P, 2], F32)
        half_tgf = sb("half_tgf", [P, 1], F32)
        id_f = sb("id_f", [P, P], F32)
        id_h = sb("id_h", [P, P], F16)
        id_b = sb("id_b", [P, P], BF16)
        lanes = sb("lanes", [P, EXPERTS], F32)
        expo = sb("expo", [P, 1], F32)

        def carver(area):
            at = [0]

            def carve(n):
                at[0] += n
                return area[:, at[0] - n:at[0]]
            return carve

        carve = carver(gu_w[:, :, :, :].rearrange("p m g f -> p (m g f)"))
        ctx_tile = [carve(C) for _ in range(2)]
        xn = [carve(C) for _ in range(2)]
        turned = [carve(2 * C) for _ in range(2)]
        qk = carve(2 * C)
        k_int = carve(C)
        k_hat = carve(C)
        k_rest = carve(C)
        q_pad = carve(2 * C).bitcast(BF16).rearrange("p (h r d) -> p h r d", h=HEADS, r=4)
        k_pad = carve(2 * C).bitcast(BF16).rearrange("p (h r d) -> p h r d", h=HEADS, r=4)
        v_ints = carve(TOKENS).bitcast(BF16).rearrange("p (m n) -> p m n", m=CH)
        stats = carve(6)
        mv = carve(2)
        vpe = carve(1)
        rstd = carve(1)
        amax = carve(2 * HEADS)
        r_step = carve(2 * HEADS)
        v_ch = o_all[:, :, :].rearrange("p t c -> p (t c)").rearrange("p (m n) -> p m n", m=CH)
        v_amax = sb("v_amax", [P, CH], F32)
        v_step = sb("v_step", [P, CH], F32)
        v_rstep = sb("v_rstep", [P, CH], F32)
        o_scale = sb("o_scale", [P, CH], F32)

        E = [sb(f"E{i}", [P, TOKENS], U16) for i in range(2)]
        PT = [sb(f"PT{i}", [P, HALF], BF16) for i in range(4)]
        mx = sb("mx", [P, 4, 2], F32)
        nmax = sb("nmax", [P, 4], F32)
        bias = sb("bias", [P, 4], F32)

        carve = carver(q_cols[:, :, :].rearrange("p h n -> p (h n)").bitcast(F32))
        att = carve(C)
        att_t = carve(C)
        x_bias = carve(C)
        xn2 = carve(C)
        xn2_t = carve(C)
        h_rows = carve(FEATS)
        h_cols = carve(BLOCKS * P).rearrange("p (b n) -> p b n", b=BLOCKS)
        th = [carve(CHUNK) for _ in range(2)]
        ga = [carve(CHUNK) for _ in range(2)]
        stats2 = carve(6)
        mv2 = carve(2)
        vpe2 = carve(1)
        rstd2 = carve(1)
        logits = carve(EXPERTS + 1)
        top_v = carve(8)
        top_i = carve(8)
        top_f = carve(8)
        gap = carve(1)
        e_gap = carve(1)
        th_sh = carve(1)
        den = carve(1)
        share = carve(2)
        pick = carve(2 * EXPERTS)
        sig = carve(1)
        r_sum = sb("r_sum", [P, TILES * HEADS], F32)
        rinv = sb("rinv", [P, TILES, HEADS], F32)

        S = [pb(f"S{i}", [P, HALF]) for i in range(3)]
        TB = pb("TB", [P, 512])
        OB = pb("OB", [P, 512])
        TB16 = TB[:, :].bitcast(F16)

        s_tile = [sem(f"tile_loaded{u}") for u in range(2)]
        s_w = sem("weights_loaded")
        s_ffw = sem("ffn_weights_loaded")
        s_id = sem("identities_made")
        s_pad = sem("pads_cleared")
        s_tg = sem("gate_tanh_done")
        s_wp = sem("weights_prepared")
        s_held = sem("waits_held")
        s_dve = sem("dve_chain")
        s_pool = sem("pool_chain")
        s_stat = sem("moments_done")
        s_rstd = sem("rstd_done")
        s_xn = sem("x_normalised")
        s_xt = sem("tile_turned")
        s_tc = sem("turned_copied")
        s_qkv = sem("qkv_projected")
        s_qkb = sem("qk_read")
        s_vev = sem("v_read")
        s_qp = sem("q_pad_filled")
        s_ki = sem("k_ints_made")
        s_kp = sem("k_pad_filled")
        s_qt = sem("q_turned")
        s_kt = sem("k_turned")
        s_qe = sem("q_cols_stored")
        s_ke = sem("k_cols_stored")
        s_vi = sem("v_ints_made")
        s_vt = sem("v_turned")
        s_vr = sem("v_rows_stored")
        s_sc = sem("scores_made")
        s_bi = sem("bias_ready")
        s_ex = sem("exp_done")
        s_tu = sem("ints_turned")
        s_ea = sem("first_half_stored")
        s_eb = sem("second_half_stored")
        s_pv = sem("pv_done")
        s_oc = sem("o_copied")
        s_ri = sem("rinv_done")
        s_an = sem("att_normalised")
        s_at = sem("att_turned")
        s_ac = sem("att_t_copied")
        s_y = sem("projected")
        s_xb = sem("x_bias_done")
        s_x1 = sem("x1_done")
        s_st2 = sem("moments2_done")
        s_rs2 = sem("rstd2_done")
        s_xn2 = sem("x1_normalised")
        s_x2t = sem("xn2_turned")
        s_x2c = sem("xn2_t_copied")
        s_lo = sem("logits_made")
        s_lc = sem("logits_read")
        s_gap = sem("gap_ready")
        s_eg = sem("gap_exp_done")
        s_co = sem("combine_ready")
        s_gu = sem("gate_up_made")
        s_th = sem("tanh_done")
        s_ga = sem("gate_read")
        s_h = sem("h_chunk_done")
        s_ht = sem("h_turned")
        s_hc = sem("h_cols_copied")
        s_dn = sem("down_done")
        s_fi = sem("final_done")
        s_out = sem("stored")

        N_W = 11
        N_FFW = 5
        N_PAD = 6

        def wait(eng, s, n):
            if isinstance(n, int) and n <= 0:
                return
            eng.wait_ge(s, n)

        def hold(eng):
            eng.sem_inc(s_held, 1)

        class Chain:

            def __init__(self, eng, s):
                self.eng, self.s, self.base, self.k = eng, s, 0, 0

            def at(self, base):
                self.base, self.k = base, 0

            def inc(self, ins):
                self.k += 1
                ins.then_inc(self.s, 1)

            def step(self, ins, held=False):
                self.inc(ins)
                self.eng.wait_ge(self.s, self.base + self.k)
                if held:
                    hold(self.eng)

        def slot(j):
            return S[(2 + j) % 3]

        def freed(t, j):
            if j >= 3:
                return 2 * HEADS * t + j - 2
            before = {0: 30, 1: 31, 2: 29}[j]
            return 2 * HEADS * (t - 1) + before + 1

        block = stack.enter_context(nc.Block())

        @block.sync
        def _(sp):
            def load(dst, src):
                sp.dma_start(dst, src).then_inc(s_w, 16)

            def tile_in(n, u):
                wait(sp, s_xt, n - 1)
                sp.dma_start(ctx_tile[u], ctx_in[n]).then_inc(s_tile[u], 16)
                sp.dma_start(x_all[:, n, :], x[n]).then_inc(s_tile[u], 16)

            tile_in(0, 0)
            tile_in(1, 1)
            load(w_qk[:, :, 0:C], w_q.rearrange("(m p) n -> p m n", p=P))
            load(w_qk[:, :, C:2 * C], w_kv.rearrange("(m p) n -> p m n", p=P)[:, :, 0:C])
            load(w_v[:, :, :], w_kv.rearrange("(m p) n -> p m n", p=P)[:, :, C:2 * C])
            load(b_qk[:, 0:C], b_q.partition_broadcast(P))
            load(b_qk[:, C:2 * C], b_kv[0:C].partition_broadcast(P))
            load(b_v[:, :], b_v_cols)
            load(w_o[:, :, :], w_p.rearrange("(m p) n -> p m n", p=P))
            load(b_o[:, :], b_p.partition_broadcast(P))
            load(w_r[:, :, :], w_route.rearrange("(m p) n -> p m n", p=P))
            load(gates[:, 0:1], g_xattn.partition_broadcast(P))
            load(gates[:, 1:2], g_ffn.partition_broadcast(P))
            with sp.Fori(1, TILES // 2) as i:
                for u in range(2):
                    tile_in(2 * i + u, u)
            sp.wait_ge(s_vr, 4)
            for m in range(CH):
                sp.dma_start(gu_w[:, m, 0, :], w_gate[m]).then_inc(s_ffw, 16)
                sp.dma_start(gu_w[:, m, 1, :], w_up[m]).then_inc(s_ffw, 16)
            sp.wait_ge(s_sc, 2 * HEADS * TILES)
            sp.dma_start(d_w[:, :, :], w_down.rearrange("(b p) n -> p b n", p=P)).then_inc(s_ffw, 16)
            with sp.Fori(0, TILES) as n:
                sp.wait_ge(s_fi, n + 1)
                sp.dma_start(out[n], x_all[:, n, :]).then_inc(s_out, 16)
            sp.wait_ge(s_out, 16 * TILES)

        @block.gpsimd
        def _(pool):
            chain = Chain(pool, s_pool)
            for ident in (id_f, id_h, id_b):
                chain.step(pool.memset(ident[:, :], 0.0))
                pool.affine_select(out=ident[:, :], in_=ident[:, :], compare_op=ALU.not_equal, fill=1.0, base=0,
                                   pattern=[[-1, P]], channel_multiplier=1).then_inc(s_id, 1)
            pool.memset(expo[:, :], -0.5).then_inc(s_id, 1)
            pool.iota(lanes[:, :], pattern=[[1, EXPERTS]], base=0, channel_multiplier=0,
                      allow_small_or_imprecise_dtypes=True).then_inc(s_id, 1)
            pool.memset(q_pad[:, :, :, :], 0.0).then_inc(s_pad, 1)
            pool.memset(k_pad[:, :, :, :], 0.0).then_inc(s_pad, 1)
            pool.memset(q_cols[0:64, 1:HEADS:2, :], 0.0).then_inc(s_pad, 1)
            pool.wait_ge(s_pad, N_PAD)
            pool.wait_ge(s_id, 5)

            def inverse_deviation(n):
                pool.wait_ge(s_stat, n + 1)
                hold(pool)
                chain.step(pool.tensor_scalar(vpe, mv[:, 1:2], LN_EPS, None, ALU.add))
                pool.tensor_tensor(rstd, vpe, expo[:, :], ALU.pow).then_inc(s_rstd, 1)

            hat = k_hat.rearrange("p (h d) -> p h d", h=HEADS)
            rest = k_rest.rearrange("p (h d) -> p h d", h=HEADS)

            def split_k(n):
                pool.wait_ge(s_ki, n + 1)
                chain.step(pool.tensor_tensor(
                    hat, k_int.rearrange("p (h d) -> p h d", h=HEADS),
                    s_all[:, n, HEADS:2 * HEADS].unsqueeze(2).broadcast_to([P, HEADS, HD]), ALU.mult))
                wait(pool, s_kt, n)
                hold(pool)
                chain.step(pool.tensor_copy(k_pad[:, :, 0, :], hat))
                chain.step(pool.tensor_tensor(rest, hat, k_pad[:, :, 0, :], ALU.subtract), held=True)
                chain.step(pool.tensor_copy(k_pad[:, :, 1, :], rest))
                pool.tensor_tensor(k_pad[:, :, 2, :], rest, k_pad[:, :, 1, :], ALU.subtract).then_inc(s_kp, 1)

            def prepare(n, more=True):
                chain.at(4 + POOL_A * n)
                if more:
                    inverse_deviation(n + 1)
                    assert chain.k == 1
                split_k(n)

            chain.at(3)
            inverse_deviation(0)
            prepare(0)
            with pool.Fori(1, TILES - 1) as n:
                prepare(n)
            prepare(TILES - 1, False)
            end_a = 4 + POOL_A * TILES - 1

            def front(n):
                wait(pool, s_x1, n)
                pool.tensor_tensor(x_bias, x_all[:, n, :], b_o[:, :], ALU.add).then_inc(s_xb, 1)
                pool.wait_ge(s_st2, n + 1)
                hold(pool)
                chain.at(end_a + n)
                chain.step(pool.tensor_scalar(vpe2, mv2[:, 1:2], LN_EPS, None, ALU.add))
                pool.tensor_tensor(rstd2, vpe2, expo[:, :], ALU.pow).then_inc(s_rs2, 1)

            pool.wait_ge(s_wp, 3)
            pool.wait_ge(s_sc, 2 * HEADS * TILES)
            front(0)
            with pool.Fori(1, TILES) as n:
                front(n)

        @block.scalar
        def _(act):
            act.wait_ge(s_w, 16 * N_W)
            act.activation(tgates[:, :], gates[:, :], ACT.Tanh).then_inc(s_tg, 1)

            def copy_turned(n, u):
                act.wait_ge(s_xt, n + 1)
                wait(act, s_qkv, n - 1)
                act.activation(turned[u], S[0][:, 512 * u:512 * u + 512], ACT.Copy).then_inc(s_tc, 1)

            def store_v(n, u):
                act.wait_ge(s_qkv, n + 1)
                for m in range(CH):
                    last = act.activation(v_ch[:, m, bass.ts(n, P)], S[2][:, 512 * u + P * m:512 * u + P * m + P],
                                          ACT.Identity, bias=b_v[:, m:m + 1])
                last.then_inc(s_vev, 1)

            def store_q(n):
                act.wait_ge(s_qt, n + 1)
                for e in range(2):
                    rows = slice(64 * e, 64 * e + 64)
                    last = act.activation(q_cols[rows, e:HEADS:2, bass.ts(n, P)],
                                          TB[:, :].bitcast(BF16)[rows, :].rearrange("p (j n) -> p j n", j=PAIRS),
                                          ACT.Copy)
                last.then_inc(s_qe, 1)

            def stage_a(n, u, more=True):
                if more:
                    copy_turned(n + 1, 1 - u)
                store_v(n, u)
                if not (isinstance(n, int) and n == 0):
                    store_q(n - 1)

            copy_turned(0, 0)
            stage_a(0, 0)
            stage_a(1, 1)
            with act.Fori(1, TILES // 2 - 1) as i:
                for u in range(2):
                    stage_a(2 * i + u, u)
            stage_a(TILES - 2, 0)
            stage_a(TILES - 1, 1, False)
            store_q(TILES - 1)

            def exp_half(t, s, half):
                U = HEADS * t + s
                j = 2 * s + half
                if half == 0:
                    act.wait_ge(s_bi, U + 1)
                    wait(act, s_tu, 2 * U - 2)
                act.activation(E[s % 2][:, :].bitcast(U8)[:, 2 * HALF * half:2 * HALF * (half + 1):2], slot(j)[:, :],
                               ACT.Exp, bias=bias[:, s % 4:s % 4 + 1], scale=s_all[:, t, s:s + 1],
                               accum_out=acc_all[:, t, j:j + 1]).then_inc(s_ex, 1)

            def store_second(t, s):
                U = HEADS * t + s
                act.wait_ge(s_tu, 2 * U + 2)
                wait(act, s_pv, 2 * U - 2)
                act.activation(PT[2 + s % 2][:, :], TB16, ACT.Copy, bias=-1024.0).then_inc(s_eb, 1)

            def attend(t, first):
                for s in range(HEADS):
                    exp_half(t, s, 0)
                    exp_half(t, s, 1)
                    if not (first and s == 0):
                        store_second(t if s else t - 1, (s - 1) % HEADS)

            attend(0, True)
            with act.Fori(1, TILES) as t:
                attend(t, False)
            store_second(TILES - 1, HEADS - 1)

            def copy_att(n):
                act.wait_ge(s_at, n + 1)
                act.activation(att_t, TB[:, 0:C], ACT.Copy).then_inc(s_ac, 1)

            def copy_xn2(n):
                act.wait_ge(s_x2t, n + 1)
                wait(act, s_gu, CHUNKS * n)
                act.activation(xn2_t, TB[:, C:2 * C], ACT.Copy).then_inc(s_x2c, 1)

            def route(n):
                act.wait_ge(s_gap, n + 1)
                act.activation(e_gap, gap, ACT.Exp)
                act.activation(th_sh, logits[:, EXPERTS:EXPERTS + 1], ACT.Tanh, scale=0.5).then_inc(s_eg, 1)

            def tanh_chunk(n, c):
                act.wait_ge(s_gu, CHUNKS * n + c + 1)
                wait(act, s_ga, CHUNKS * n + c - 1)
                act.activation(th[c % 2], S[0][:, 512 * (c % 2):512 * (c % 2) + CHUNK], ACT.Tanh,
                               scale=0.5).then_inc(s_th, 1)

            def copy_h(n, g):
                a, b = GROUPS[g]
                rows = LAST_BLOCK if b - a == 1 else P
                act.wait_ge(s_ht, len(GROUPS) * n + g + 1)
                wait(act, s_dn, n)
                act.activation(h_cols[0:rows, a:b, :],
                               S[2][0:rows, 512 * (g % 2):512 * (g % 2) + P * (b - a)].rearrange(
                                   "p (b n) -> p b n", b=b - a), ACT.Copy).then_inc(s_hc, 1)

            def ffn(n, front):
                tanh_chunk(n, 0)
                tanh_chunk(n, 1)
                if front:
                    copy_att(n + 1)
                tanh_chunk(n, 2)
                copy_h(n, 0)
                tanh_chunk(n, 3)
                copy_h(n, 1)
                tanh_chunk(n, 4)
                tanh_chunk(n, 5)
                copy_h(n, 2)
                if front:
                    copy_xn2(n + 1)
                copy_h(n, 3)
                copy_h(n, 4)
                if front:
                    route(n + 1)

            copy_att(0)
            copy_xn2(0)
            route(0)
            ffn(0, True)
            with act.Fori(1, TILES - 1) as n:
                ffn(n, True)
            ffn(TILES - 1, False)

        @block.vector
        def _(dve):
            chain = Chain(dve, s_dve)
            dve.memset(q_cols[64:128, 0:HEADS:2, :], 0.0).then_inc(s_pad, 1)
            for i in range(2):
                dve.memset(E[i][:, :], MARK).then_inc(s_pad, 1)
            dve.wait_ge(s_w, 16 * N_W)
            dve.tensor_scalar(w_qk[:, :, 0:C], w_qk[:, :, 0:C], Q_SCALE, None, ALU.mult).then_inc(s_wp, 1)
            chain.step(dve.tensor_scalar(b_qk[:, 0:C], b_qk[:, 0:C], Q_SCALE, None, ALU.mult))
            dve.wait_ge(s_tg, 1)
            dve.tensor_scalar(b_o[:, :], b_o[:, :], tgates[:, 0:1], None, ALU.mult).then_inc(s_wp, 1)
            chain.step(dve.tensor_scalar(half_tgf[:, :], tgates[:, 1:2], 0.5, None, ALU.mult))
            BASE_A = 2

            def normalise(n, u):
                dve.wait_ge(s_tile[u], 32 * ((n - u) // 2 + 1) if isinstance(n, int) else 16 * (n - u) + 32)
                hold(dve)
                chain.step(dve.bn_stats(stats, x_all[:, n, :]), held=True)
                dve.bn_aggr(mv, stats).then_inc(s_stat, 1)
                dve.wait_ge(s_stat, n + 1)
                dve.wait_ge(s_rstd, n + 1)
                wait(dve, s_xt, n - 1)
                dve.tensor_scalar(xn[u], x_all[:, n, :], mv[:, 0:1], rstd, ALU.subtract,
                                  ALU.mult).then_inc(s_xn, 1)

            def quantise(n, u):
                wait(dve, s_qp, n)
                dve.wait_ge(s_qkv, n + 1)
                dve.tensor_tensor(qk, S[1][:, 512 * u:512 * u + 512], b_qk[:, :], ALU.add).then_inc(s_qkb, 1)
                dve.wait_ge(s_qkb, n + 1)
                heads = qk.rearrange("p (h d) -> p h d", h=2 * HEADS)
                chain.step(dve.tensor_reduce(amax, heads, axis=AX.X, op=ALU.max,
                                             apply_absolute_value=True))
                chain.step(dve.tensor_scalar(s_all[:, n, :], amax, 1.0 / 127.0, 1e-8, ALU.mult, ALU.max))
                chain.inc(dve.tensor_scalar(nsq_all[:, n, :], s_all[:, n, 0:HEADS], -1.0, None, ALU.mult))
                chain.step(dve.reciprocal(r_step, s_all[:, n, :]))
                chain.step(dve.tensor_tensor(heads, heads, r_step.unsqueeze(2).broadcast_to(
                    [P, 2 * HEADS, HD]), ALU.mult))
                wait(dve, s_kp, n)
                dve.tensor_scalar(k_int, qk[:, C:2 * C], ROUND, -ROUND, ALU.add, ALU.add).then_inc(s_ki, 1)
                wait(dve, s_qt, n)
                dve.tensor_scalar(
                    q_pad[:, :, 0:3, :],
                    qk[:, 0:C].rearrange("p (h d) -> p h d", h=HEADS).unsqueeze(2).broadcast_to([P, HEADS, 3, HD]),
                    ROUND, -ROUND, ALU.add, ALU.add).then_inc(s_qp, 1)

            def store_k(n):
                dve.wait_ge(s_kt, n + 1)
                dve.tensor_copy(k_cols[:, :, bass.ts(n, P)], OB[:, :].bitcast(BF16).rearrange(
                    "p (j n) -> p j n", j=PAIRS)).then_inc(s_ke, 1)

            def stage_a(n, u, more=True):
                if more:
                    chain.at(BASE_A + 1 + DVE_A * n)
                    normalise(n + 1, 1 - u)
                    quantise(n, u)
                    assert chain.k == DVE_A
                else:
                    chain.at(BASE_A + 1 + DVE_A * n)
                    quantise(n, u)
                if not (isinstance(n, int) and n == 0):
                    store_k(n - 1)

            chain.at(BASE_A)
            normalise(0, 0)
            stage_a(0, 0)
            stage_a(1, 1)
            with dve.Fori(1, TILES // 2 - 1) as i:
                for u in range(2):
                    stage_a(2 * i + u, u)
            stage_a(TILES - 2, 0)
            stage_a(TILES - 1, 1, False)
            store_k(TILES - 1)

            chain.at(BASE_A + DVE_A * TILES)
            dve.wait_ge(s_vev, TILES)
            chain.step(dve.tensor_reduce(v_amax[:, :], v_ch, axis=AX.X, op=ALU.max, apply_absolute_value=True))
            chain.step(dve.tensor_scalar(v_step[:, :], v_amax[:, :], 1.0 / 127.0, 1e-8, ALU.mult, ALU.max))
            chain.step(dve.reciprocal(v_rstep[:, :], v_step[:, :]))
            for m in range(CH):
                chain.step(dve.tensor_scalar(v_ch[:, m, :], v_ch[:, m, :], v_rstep[:, m:m + 1], ROUND, ALU.mult,
                                             ALU.add))
                dve.tensor_scalar(v_ints[:, m, :], v_ch[:, m, :], -ROUND, None, ALU.add).then_inc(s_vi, 1)
            chain.step(dve.tensor_scalar(o_scale[:, :], v_step[:, :], tgates[:, 0:1], None, ALU.mult))
            for m in range(CH):
                last = dve.tensor_scalar(w_o[:, m, :], w_o[:, m, :], o_scale[:, m:m + 1], None, ALU.mult)
            last.then_inc(s_wp, 1)
            for k in range(4):
                bank = TB if k % 2 == 0 else OB
                dve.wait_ge(s_vt, k + 1)
                dve.tensor_copy(v_rows[:, 4 * k:4 * k + 4, :].rearrange("p a c -> p (a c)"),
                                bank[:, :].bitcast(BF16)).then_inc(s_vr, 1)

            base_b = BASE_A + DVE_A * TILES + 6

            def max_half(t, s, half):
                U = HEADS * t + s
                dve.wait_ge(s_sc, 2 * U + half + 1)
                chain.inc(dve.tensor_reduce(mx[:, s % 4, half:half + 1], slot(2 * s + half)[:, :], axis=AX.X,
                                            op=ALU.max))

            def make_bias(t, s):
                U = HEADS * t + s
                dve.wait_ge(s_dve, base_b + 3 * U + 2)
                dve.tensor_scalar(nmax[:, s % 4:s % 4 + 1], mx[:, s % 4, 0:1], mx[:, s % 4, 1:2],
                                  nsq_all[:, t, s:s + 1], ALU.max, ALU.mult).then_inc(s_dve, 1)
                dve.wait_ge(s_dve, base_b + 3 * U + 3)
                dve.tensor_scalar(bias[:, s % 4:s % 4 + 1], nmax[:, s % 4:s % 4 + 1], LN255, None,
                                  ALU.add).then_inc(s_bi, 1)

            def store_first(t, s):
                U = HEADS * t + s
                dve.wait_ge(s_tu, 2 * U + 1)
                wait(dve, s_pv, 2 * U - 3)
                dve.tensor_scalar(PT[s % 2][:, :], TB16, -1024.0, None, ALU.add).then_inc(s_ea, 1)

            def copy_o(t):
                dve.wait_ge(s_pv, 2 * HEADS * (t + 1))
                dve.tensor_copy(o_all[:, t, :], OB[:, 0:C]).then_inc(s_oc, 1)

            def attend(t, first, last):
                for s in range(HEADS):
                    if s + 1 < HEADS:
                        max_half(t, s + 1, 1)
                        make_bias(t, s + 1)
                        if s + 2 < HEADS:
                            max_half(t, s + 2, 0)
                    elif not last:
                        max_half(t + 1, 0, 0)
                        max_half(t + 1, 0, 1)
                        make_bias(t + 1, 0)
                        max_half(t + 1, 1, 0)
                    if s == 0 and not first:
                        copy_o(t - 1)
                    store_first(t, s)

            max_half(0, 0, 0)
            max_half(0, 0, 1)
            make_bias(0, 0)
            max_half(0, 1, 0)
            attend(0, True, False)
            with dve.Fori(1, TILES - 1) as t:
                attend(t, False, False)
            attend(TILES - 1, False, True)
            copy_o(TILES - 1)

            base_c = base_b + 3 * HEADS * TILES
            acc = acc_all[:, :, :].rearrange("p t (h e) -> p (t h) e", e=2)
            dve.wait_ge(s_ex, 2 * HEADS * TILES)
            chain.at(base_c)
            chain.step(dve.tensor_tensor(r_sum[:, :], acc[:, :, 0], acc[:, :, 1], ALU.add))
            dve.reciprocal(rinv[:, :, :].rearrange("p t h -> p (t h)"), r_sum[:, :]).then_inc(s_ri, 1)
            dve.wait_ge(s_ri, 1)
            dve.wait_ge(s_oc, TILES)
            base_c += 1

            def normalise_att(n):
                wait(dve, s_at, n)
                dve.tensor_tensor(att.rearrange("p (h d) -> p h d", h=HEADS),
                                  o_all[:, n, :].rearrange("p (h d) -> p h d", h=HEADS),
                                  rinv[:, n, :].unsqueeze(2).broadcast_to([P, HEADS, HD]),
                                  ALU.mult).then_inc(s_an, 1)

            def residual(n):
                dve.wait_ge(s_y, n + 1)
                dve.wait_ge(s_xb, n + 1)
                dve.tensor_tensor(x_all[:, n, :], OB[:, C:2 * C], x_bias, ALU.add).then_inc(s_x1, 1)
                dve.wait_ge(s_x1, n + 1)
                hold(dve)
                chain.step(dve.bn_stats(stats2, x_all[:, n, :]), held=True)
                dve.bn_aggr(mv2, stats2).then_inc(s_st2, 1)

            def normalise_x1(n):
                dve.wait_ge(s_st2, n + 1)
                dve.wait_ge(s_rs2, n + 1)
                wait(dve, s_x2t, n)
                dve.tensor_scalar(xn2, x_all[:, n, :], mv2[:, 0:1], rstd2, ALU.subtract, ALU.mult).then_inc(s_xn2, 1)

            def route(n):
                dve.wait_ge(s_lo, n + 1)
                dve.tensor_copy(logits, TB[:, 0:EXPERTS + 1]).then_inc(s_lc, 1)
                dve.wait_ge(s_lc, n + 1)
                hold(dve)
                chain.step(dve.max(top_v, logits[:, 0:EXPERTS]), held=True)
                chain.step(dve.max_index(top_i.bitcast(U32), top_v, logits[:, 0:EXPERTS]))
                chain.step(dve.tensor_copy(top_f, top_i.bitcast(U32)))
                dve.tensor_tensor(gap, top_v[:, 1:2], top_v[:, 0:1], ALU.subtract).then_inc(s_gap, 1)
                dve.wait_ge(s_eg, n + 1)
                chain.step(dve.tensor_scalar(den, e_gap, 1.0, None, ALU.add))
                chain.step(dve.reciprocal(share[:, 0:1], den))
                chain.step(dve.tensor_scalar(share[:, 1:2], e_gap, share[:, 0:1], None, ALU.mult))
                chain.step(dve.tensor_scalar(share, share, half_tgf[:, :], None, ALU.mult))
                for k in range(2):
                    chain.step(dve.tensor_scalar(pick[:, EXPERTS * k:EXPERTS * (k + 1)], lanes[:, :],
                                                 top_f[:, k:k + 1], share[:, k:k + 1], ALU.is_equal, ALU.mult))
                chain.step(dve.tensor_scalar(sig, th_sh, 0.5, 0.5, ALU.mult, ALU.add))
                chain.step(dve.tensor_tensor(comb_all[:, n, 0:EXPERTS], pick[:, 0:EXPERTS],
                                             pick[:, EXPERTS:2 * EXPERTS], ALU.add))
                dve.tensor_scalar(comb_all[:, n, EXPERTS:EXPERTS + 1], sig, half_tgf[:, :], None,
                                  ALU.mult).then_inc(s_co, 1)

            def chunk(n, c):
                G = S[0][:, 512 * (c % 2):512 * (c % 2) + CHUNK]
                Up = S[1][:, 512 * (c % 2):512 * (c % 2) + CHUNK]
                dve.wait_ge(s_th, CHUNKS * n + c + 1)
                dve.scalar_tensor_tensor(out=ga[c % 2], in0=th[c % 2], scalar=1.0, in1=G, op0=ALU.add,
                                         op1=ALU.mult).then_inc(s_ga, 1)
                dve.wait_ge(s_ga, CHUNKS * n + c + 1)
                if c == 0:
                    dve.wait_ge(s_co, n + 1)
                    wait(dve, s_ht, len(GROUPS) * n)
                for e, a, b in ([(2 * c, 0, I_MOE), (2 * c + 1, I_MOE, CHUNK)] if 2 * c < EXPERTS
                                else [(EXPERTS, 0, CHUNK)]):
                    last = dve.scalar_tensor_tensor(
                        out=h_rows[:, CHUNK * c + a:CHUNK * c + b], in0=ga[c % 2][:, a:b],
                        scalar=comb_all[:, n, e:e + 1], in1=Up[:, a:b], op0=ALU.mult, op1=ALU.mult)
                last.then_inc(s_h, 1)

            def final(n):
                dve.wait_ge(s_dn, n + 1)
                dve.tensor_tensor(x_all[:, n, :], x_all[:, n, :], OB[:, 0:C], ALU.add).then_inc(s_fi, 1)

            def ffn(n, front):
                chain.at(base_c + DVE_FRONT * (n + 1))
                chunk(n, 0)
                if front:
                    normalise_att(n + 1)
                chunk(n, 1)
                chunk(n, 2)
                if front:
                    residual(n + 1)
                chunk(n, 3)
                if front:
                    normalise_x1(n + 1)
                chunk(n, 4)
                chunk(n, 5)
                if front:
                    route(n + 1)
                    assert chain.k == DVE_FRONT, chain.k
                final(n)

            chain.at(base_c)
            normalise_att(0)
            residual(0)
            normalise_x1(0)
            route(0)
            ffn(0, True)
            with dve.Fori(1, TILES - 1) as n:
                ffn(n, True)
            ffn(TILES - 1, False)

        @block.tensor
        def _(pe):
            def turn_tile(n, u):
                dve_and_dma = 32 * ((n - u) // 2 + 1) if isinstance(n, int) else 16 * (n - u) + 32
                pe.wait_ge(s_tile[u], dve_and_dma)
                pe.wait_ge(s_xn, n + 1)
                wait(pe, s_tc, n - 1)
                for m in range(CH):
                    pe.transpose(S[0][:, 512 * u + P * m:512 * u + P * m + P], xn[u][:, bass.ts(m, P)], id_f[:, :])
                for m in range(CH):
                    last = pe.transpose(S[0][:, 512 * u + C + P * m:512 * u + C + P * m + P],
                                        ctx_tile[u][:, bass.ts(m, P)], id_f[:, :])
                last.then_inc(s_xt, 1)

            def project(n, u):
                pe.wait_ge(s_tc, n + 1)
                wait(pe, s_qkb, n - 1)
                wait(pe, s_vev, n - 1)
                for side in range(2):
                    for m in range(CH):
                        pe.matmul(S[1][:, 512 * u + C * side:512 * u + C * side + C],
                                  turned[u][:, C * side + P * m:C * side + P * m + P],
                                  w_qk[:, m, C * side:C * side + C], start=(m == 0), stop=(m == CH - 1))
                for mo in range(CH):
                    for m in range(CH):
                        last = pe.matmul(S[2][:, 512 * u + P * mo:512 * u + P * mo + P],
                                         w_v[:, m, bass.ts(mo, P)], turned[u][:, C + P * m:C + P * m + P],
                                         start=(m == 0), stop=(m == CH - 1))
                last.then_inc(s_qkv, 1)

            def turn_pads(n):
                pe.wait_ge(s_qp, n + 1)
                wait(pe, s_qe, n)
                for j in range(PAIRS):
                    last = pe.transpose(TB[:, :].bitcast(BF16)[:, bass.ts(j, P)],
                                        q_pad[:, 2 * j:2 * j + 2, :, :].rearrange("p h r d -> p (h r d)"),
                                        id_b[:, :])
                last.then_inc(s_qt, 1)
                pe.wait_ge(s_kp, n + 1)
                wait(pe, s_ke, n)
                for j in range(PAIRS):
                    last = pe.transpose(OB[:, :].bitcast(BF16)[:, bass.ts(j, P)],
                                        k_pad[:, 2 * j:2 * j + 2, :, :].rearrange("p h r d -> p (h r d)"),
                                        id_b[:, :])
                last.then_inc(s_kt, 1)

            def stage_a(n, u, more=True):
                if more:
                    turn_tile(n + 1, 1 - u)
                project(n, u)
                if not (isinstance(n, int) and n == 0):
                    turn_pads(n - 1)

            pe.wait_ge(s_id, 5)
            pe.wait_ge(s_pad, N_PAD)
            turn_tile(0, 0)
            pe.wait_ge(s_w, 16 * N_W)
            pe.wait_ge(s_wp, 1)
            stage_a(0, 0)
            stage_a(1, 1)
            with pe.Fori(1, TILES // 2 - 1) as i:
                for u in range(2):
                    stage_a(2 * i + u, u)
            stage_a(TILES - 2, 0)
            stage_a(TILES - 1, 1, False)
            turn_pads(TILES - 1)

            def scores(t, j):
                s, half = j // 2, j % 2
                wait(pe, s_ex, freed(t, j))
                for b in range(2):
                    last = pe.matmul(slot(j)[:, bass.ts(b, 512)], q_cols[:, s, bass.ts(t, P)],
                                     k_cols[:, s // 2, HALF * half + 512 * b:HALF * half + 512 * b + 512],
                                     start=True, stop=True)
                last.then_inc(s_sc, 1)

            def turn_ints(t, s, half):
                U = HEADS * t + s
                pe.wait_ge(s_ex, 2 * U + half + 1)
                if half == 0:
                    wait(pe, s_eb, U)
                else:
                    pe.wait_ge(s_ea, U + 1)
                for k in range(KTH):
                    kt = KTH * half + k
                    last = pe.transpose(TB16[:, bass.ts(k, P)], E[s % 2][:, :].bitcast(F16)[:, bass.ts(kt, P)],
                                        id_h[:, :])
                last.then_inc(s_tu, 1)

            def times_v(t, s, half):
                U = HEADS * t + s
                if half == 0:
                    pe.wait_ge(s_ea, U + 1)
                    if s == 0:
                        wait(pe, s_oc, t)
                else:
                    pe.wait_ge(s_eb, U + 1)
                ints = PT[2 * half + s % 2]
                for k in range(KTH):
                    kt = KTH * half + k
                    last = pe.matmul(OB[:, HD * s:HD * s + HD], ints[:, bass.ts(k, P)],
                                     v_rows[:, kt, HD * s:HD * s + HD], start=(kt == 0), stop=(kt == KT - 1))
                last.then_inc(s_pv, 1)

            def attend(t, first, last):
                for s in range(HEADS):
                    if s + 1 < HEADS:
                        scores(t, 2 * s + 3)
                        if s + 2 < HEADS:
                            scores(t, 2 * s + 4)
                    elif not last:
                        for j in range(3):
                            scores(t + 1, j)
                    turn_ints(t, s, 0)
                    if not (first and s == 0):
                        times_v(t if s else t - 1, (s - 1) % HEADS, 1)
                    turn_ints(t, s, 1)
                    times_v(t, s, 0)

            pe.wait_ge(s_qe, TILES)
            pe.wait_ge(s_ke, TILES)
            pe.wait_ge(s_qkb, TILES)
            pe.wait_ge(s_vev, TILES)
            for j in range(3):
                scores(0, j)
            pe.wait_ge(s_vi, CH)
            for k in range(4):
                bank = TB if k % 2 == 0 else OB
                wait(pe, s_vr, k - 1)
                for i in range(4):
                    for m in range(CH):
                        last = pe.transpose(bank[:, :].bitcast(BF16)[:, C * i + P * m:C * i + P * m + P],
                                            v_ints[:, m, bass.ts(4 * k + i, P)], id_b[:, :])
                last.then_inc(s_vt, 1)
            pe.wait_ge(s_vr, 4)
            attend(0, True, False)
            with pe.Fori(1, TILES - 1) as t:
                attend(t, False, False)
            attend(TILES - 1, False, True)
            times_v(TILES - 1, HEADS - 1, 1)

            def turn_att(n):
                pe.wait_ge(s_an, n + 1)
                wait(pe, s_x2c, n)
                wait(pe, s_lc, n)
                for m in range(CH):
                    last = pe.transpose(TB[:, bass.ts(m, P)], att[:, bass.ts(m, P)], id_f[:, :])
                last.then_inc(s_at, 1)

            def project_att(n):
                pe.wait_ge(s_ac, n + 1)
                wait(pe, s_fi, n - 1)
                for m in range(CH):
                    last = pe.matmul(OB[:, C:2 * C], att_t[:, bass.ts(m, P)], w_o[:, m, :], start=(m == 0),
                                     stop=(m == CH - 1))
                last.then_inc(s_y, 1)

            def turn_xn2(n):
                pe.wait_ge(s_xn2, n + 1)
                for m in range(CH):
                    last = pe.transpose(TB[:, C + P * m:C + P * m + P], xn2[:, bass.ts(m, P)], id_f[:, :])
                last.then_inc(s_x2t, 1)

            def route(n):
                pe.wait_ge(s_x2c, n + 1)
                for m in range(CH):
                    last = pe.matmul(TB[:, 0:EXPERTS + 1], xn2_t[:, bass.ts(m, P)], w_r[:, m, :], start=(m == 0),
                                     stop=(m == CH - 1))
                last.then_inc(s_lo, 1)

            def gate_up(n, c):
                if c == 0:
                    pe.wait_ge(s_x2c, n + 1)
                wait(pe, s_ga, CHUNKS * n + c - 1)
                wait(pe, s_h, CHUNKS * n + c - 1)
                for side in range(2):
                    for m in range(CH):
                        last = pe.matmul(S[side][:, 512 * (c % 2):512 * (c % 2) + CHUNK],
                                         xn2_t[:, bass.ts(m, P)], gu_w[:, m, side, CHUNK * c:CHUNK * (c + 1)],
                                         start=(m == 0), stop=(m == CH - 1))
                last.then_inc(s_gu, 1)

            def turn_h(n, g):
                a, b = GROUPS[g]
                done = -(-min(P * b, FEATS) // CHUNK)
                pe.wait_ge(s_h, CHUNKS * n + done)
                wait(pe, s_hc, len(GROUPS) * n + (g - 1 if g >= 2 else 0))
                if b - a == 1:
                    hold(pe)
                for k in range(a, b):
                    w = min(P, FEATS - P * k)
                    last = pe.transpose(S[2][0:w, 512 * (g % 2) + P * (k - a):512 * (g % 2) + P * (k - a) + P],
                                        h_rows[:, P * k:P * k + w], id_f[:, :])
                last.then_inc(s_ht, 1)

            def down(n, g, front):
                pe.wait_ge(s_hc, len(GROUPS) * n + g + 1)
                if g == 0 and front:
                    pe.wait_ge(s_x1, n + 2)
                for k in range(*GROUPS[g]):
                    w = min(P, FEATS - P * k)
                    last = pe.matmul(OB[:, 0:C], h_cols[0:w, k, :], d_w[0:w, k, :], start=(k == 0),
                                     stop=(k == BLOCKS - 1))
                if g == len(GROUPS) - 1:
                    last.then_inc(s_dn, 1)

            def ffn(n, front):
                gate_up(n, 0)
                gate_up(n, 1)
                if front:
                    turn_att(n + 1)
                gate_up(n, 2)
                if front:
                    project_att(n + 1)
                turn_h(n, 0)
                gate_up(n, 3)
                down(n, 0, front)
                turn_h(n, 1)
                gate_up(n, 4)
                down(n, 1, front)
                gate_up(n, 5)
                turn_h(n, 2)
                if front:
                    turn_xn2(n + 1)
                down(n, 2, front)
                turn_h(n, 3)
                turn_h(n, 4)
                if front:
                    route(n + 1)
                down(n, 3, front)
                down(n, 4, front)

            pe.wait_ge(s_wp, 3)
            pe.wait_ge(s_oc, TILES)
            turn_att(0)
            project_att(0)
            turn_xn2(0)
            route(0)
            pe.wait_ge(s_ffw, 16 * N_FFW)
            ffn(0, True)
            with pe.Fori(1, TILES - 1) as n:
                ffn(n, True)
            ffn(TILES - 1, False)


def kernel(**inputs):
    import numpy as np
    import concourse.bacc as bacc
    from concourse import mybir as mb
    from concourse.bass_utils import run_bass_kernel_spmd

    a = {k: np.asarray(v) for k, v in inputs.items()}
    gu = a["L0_ffn_gate_up_proj"]
    gate = np.concatenate([gu[:, :I_MOE].reshape(-1, C), a["L0_ffn_sh_gate_w"]])
    up = np.concatenate([gu[:, I_MOE:].reshape(-1, C), a["L0_ffn_sh_up_w"]])
    down = np.concatenate([a["L0_ffn_down_proj"].transpose(0, 2, 1).reshape(-1, C), a["L0_ffn_sh_down_w"].T])
    laid = {
        "x": a["x"].reshape(TILES, P, C),
        "ctx": a["ctx_2048"].reshape(TILES, P, C),
        "g_xattn": a["g_xattn"],
        "g_ffn": a["g_ffn"],
        "w_q": a["L0_xattn_Wq"],
        "b_q": a["L0_xattn_bq"],
        "w_kv": a["L0_xattn_Wkv"],
        "b_kv": a["L0_xattn_bkv"],
        "b_v_cols": a["L0_xattn_bkv"][C:].reshape(CH, P).T,
        "w_p": a["L0_xattn_Wp"],
        "b_p": a["L0_xattn_bp"],
        "w_route": np.concatenate([a["L0_ffn_router_weight"], a["L0_ffn_shared_gate_w"]]).T,
        "w_gate": gate.T.reshape(CH, P, FEATS),
        "w_up": up.T.reshape(CH, P, FEATS),
        "w_down": np.concatenate([down, np.zeros((BLOCKS * P - FEATS, C), down.dtype)]),
    }
    nc = bacc.Bacc("TRN2", target_bir_lowering=False, num_devices=1)
    arrays, args = {}, []
    for name, v in laid.items():
        arrays[f"in_{name}"] = np.ascontiguousarray(v)
        args.append(nc.dram_tensor(f"in_{name}", v.shape, mb.dt.from_np(v.dtype), kind="ExternalInput").ap())
    out = nc.dram_tensor("out_y", (TILES, P, C), mb.dt.float32, kind="ExternalOutput").ap()
    build(nc, *args, out)
    r = run_bass_kernel_spmd(nc, [arrays], core_ids=[0])
    return r.results[0]["out_y"].reshape(a["x"].shape)
```

```python
import concourse.bass as bass
from concourse import mybir
from contextlib import ExitStack
import math

F32 = mybir.dt.float32
BF16 = mybir.dt.bfloat16
F16 = mybir.dt.float16
U16 = mybir.dt.uint16
U8 = mybir.dt.uint8
U32 = mybir.dt.uint32
ALU = mybir.AluOpType
ACT = mybir.ActivationFunctionType
AX = mybir.AxisListType

P = 128
TOKENS = 2048
TILES = TOKENS // P
C = 256
CH = C // P
HEADS = 16
HD = C // HEADS
PAIRS = HEADS // 2
HALF = TOKENS // 2
KT = TOKENS // P
KTH = KT // 2
QUARTERS = TOKENS // 512
XPARTS = 4
UNITS = TILES * HEADS
EXPERTS = 8
I_MOE = 176
I_SH = 704
FEATS = EXPERTS * I_MOE + I_SH
CHUNK = 2 * I_MOE
CHUNKS = FEATS // CHUNK
BLOCKS = -(-FEATS // P)
LAST_BLOCK = FEATS - (BLOCKS - 1) * P
GROUPS = [(g, min(g + 4, BLOCKS)) for g in range(0, BLOCKS, 4)]
ROUND = 1.5 * 2.0 ** 23
MARK = 0x6400
LN_EPS = 1e-5
Q_SCALE = 1.0 / math.sqrt(HD)
LN255 = math.log(255.0)

DVE_A, POOL_A = 6, 4
DVE_FRONT = 12


def build(nc, x, ctx_in, g_xattn, g_ffn, w_q, b_q, w_kv, b_kv, b_v_cols, w_p, b_p, w_route, w_gate, w_up, w_down, out):
    stack = ExitStack()
    with stack:
        def sb(name, shape, dt):
            return stack.enter_context(nc.sbuf_tensor(name, shape, dt))

        def pb(name, shape, dt=F32):
            return stack.enter_context(nc.psum_tensor(name, shape, dt))

        def sem(name):
            return stack.enter_context(nc.semaphore(name))

        x_all = sb("x_all", [P, TILES, C], F32)
        k_cols = sb("k_cols", [P, PAIRS, TOKENS], BF16)
        q_cols = sb("q_cols", [P, HEADS, TOKENS], BF16)
        v_rows = sb("v_rows", [P, KT, C], BF16)
        o_all = sb("o_all", [P, TILES, C], F32)
        s_all = sb("s_all", [P, TILES, 2 * HEADS], F32)
        nsq_all = sb("nsq_all", [P, TILES, HEADS], F32)
        acc_all = sb("acc_all", [P, TILES, 2 * HEADS], F32)
        comb_all = sb("comb_all", [P, TILES, EXPERTS + 1], F32)
        gu_w = sb("gu_w", [P, CH, 2, FEATS], F32)
        d_w = k_cols[:, :, :].rearrange("p j n -> p (j n)").bitcast(F32)[:, 0:BLOCKS * C].rearrange(
            "p (b n) -> p b n", b=BLOCKS)

        w_qk = sb("w_qk", [P, CH, 2 * C], F32)
        w_v = sb("w_v", [P, CH, C], F32)
        w_o = sb("w_o", [P, CH, C], F32)
        w_r = sb("w_r", [P, CH, EXPERTS + 1], F32)
        b_qk = sb("b_qk", [P, 2 * C], F32)
        b_v = sb("b_v", [P, CH], F32)
        b_o = sb("b_o", [P, C], F32)
        gates = sb("gates", [P, 2], F32)
        tgates = sb("tgates", [P, 2], F32)
        half_tgf = sb("half_tgf", [P, 1], F32)
        id_f = sb("id_f", [P, P], F32)
        id_h = sb("id_h", [P, P], F16)
        id_b = sb("id_b", [P, P], BF16)
        lanes = sb("lanes", [P, EXPERTS], F32)
        expo = sb("expo", [P, TILES], F32)

        def carver(area):
            at = [0]

            def carve(n):
                at[0] += n
                return area[:, at[0] - n:at[0]]
            return carve

        carve = carver(gu_w[:, :, :, :].rearrange("p m g f -> p (m g f)"))
        ctx_tile = [carve(C) for _ in range(2)]
        xn = [carve(C) for _ in range(2)]
        turned = [carve(2 * C) for _ in range(2)]
        qk = carve(2 * C)
        k_int = [carve(C) for _ in range(2)]
        k_hat = carve(C)
        k_rest = carve(C)
        q_pad = [carve(2 * C).bitcast(BF16).rearrange("p (h r d) -> p h r d", h=HEADS, r=4) for _ in range(2)]
        k_pad = [carve(2 * C).bitcast(BF16).rearrange("p (h r d) -> p h r d", h=HEADS, r=4) for _ in range(2)]
        v_ints = carve(TOKENS).bitcast(BF16).rearrange("p (m n) -> p m n", m=CH)
        stats = carve(6 * TILES).rearrange("p (t k) -> p t k", t=TILES)
        mv = carve(2 * TILES).rearrange("p (t k) -> p t k", t=TILES)
        vpe = carve(TILES)
        rstd = carve(TILES).rearrange("p (t k) -> p t k", t=TILES)
        v_amax_t = carve(CH * TILES).rearrange("p (t m) -> p t m", t=TILES)
        amax = carve(2 * HEADS)
        r_step = carve(2 * HEADS)
        v_ch = o_all[:, :, :].rearrange("p t c -> p (t c)").rearrange("p (m n) -> p m n", m=CH)
        v_amax = sb("v_amax", [P, CH], F32)
        v_step = sb("v_step", [P, CH], F32)
        v_rstep = sb("v_rstep", [P, CH], F32)
        o_scale = sb("o_scale", [P, CH], F32)

        E = [sb(f"E{i}", [P, TOKENS], U16) for i in range(2)]
        PT = [sb(f"PT{i}", [P, HALF], BF16) for i in range(4)]
        mx = sb("mx", [P, 4, QUARTERS], F32)
        nmax = sb("nmax", [P, 4], F32)
        bias = sb("bias", [P, 4], F32)

        carve = carver(q_cols[:, :, :].rearrange("p h n -> p (h n)").bitcast(F32))
        att = carve(C)
        att_t = carve(C)
        x_bias = carve(C)
        xn2 = carve(C)
        xn2_t = carve(C)
        h_rows = carve(FEATS)
        h_cols = carve(BLOCKS * P).rearrange("p (b n) -> p b n", b=BLOCKS)
        th = [carve(CHUNK) for _ in range(2)]
        ga = [carve(CHUNK) for _ in range(2)]
        stats2 = carve(6)
        mv2 = carve(2)
        vpe2 = carve(1)
        rstd2 = carve(1)
        logits = carve(EXPERTS + 1)
        top_v = carve(8)
        top_i = carve(8)
        top_f = carve(8)
        gap = carve(1)
        e_gap = carve(1)
        th_sh = carve(1)
        den = carve(1)
        share = carve(2)
        pick = carve(2 * EXPERTS)
        sig = carve(1)
        r_sum = sb("r_sum", [P, TILES * HEADS], F32)
        rinv = sb("rinv", [P, TILES, HEADS], F32)

        X = [pb(f"X{i}", [P, HALF]) for i in range(2)]
        M = [pb(f"M{i}", [P, 512]) for i in range(2)]
        TB = pb("TB", [P, 512])
        OB = pb("OB", [P, 512])
        TB16 = TB[:, :].bitcast(F16)

        s_ctx = [sem(f"ctx_loaded{u}") for u in range(2)]
        s_x = [sem(f"x_loaded{i}") for i in range(XPARTS)]
        s_w = sem("weights_loaded")
        s_ffw = sem("ffn_weights_loaded")
        s_id = sem("identities_made")
        s_pad = sem("pads_cleared")
        s_mark = sem("marks_set")
        s_zero = sem("other_heads_cleared")
        s_tg = sem("gate_tanh_done")
        s_wp = sem("weights_prepared")
        s_held = sem("waits_held")
        s_dve = sem("dve_chain")
        s_pool = sem("pool_chain")
        s_stat = sem("moments_done")
        s_rstd = sem("rstd_done")
        s_xn = sem("x_normalised")
        s_xt = sem("tile_turned")
        s_tc = sem("turned_copied")
        s_qkv = sem("qkv_projected")
        s_qkb = sem("qk_read")
        s_vev = sem("v_read")
        s_qp = sem("q_pad_filled")
        s_ki = sem("k_ints_made")
        s_kp = sem("k_pad_filled")
        s_qt = sem("q_turned")
        s_kt = sem("k_turned")
        s_qe = sem("q_cols_stored")
        s_ke = sem("k_cols_stored")
        s_vi = sem("v_ints_made")
        s_vt = sem("v_turned")
        s_vr = sem("v_rows_stored")
        s_ms = sem("max_scores_made")
        s_mr = sem("max_scores_reduced")
        s_nm = sem("row_max_ready")
        s_xs = sem("exp_scores_made")
        s_bi = sem("bias_ready")
        s_ex = sem("exp_done")
        s_tu = sem("ints_turned")
        s_ea = sem("first_half_stored")
        s_eb = sem("second_half_stored")
        s_pv = sem("pv_done")
        s_oc = sem("o_copied")
        s_ri = sem("rinv_done")
        s_an = sem("att_normalised")
        s_at = sem("att_turned")
        s_ac = sem("att_t_copied")
        s_y = sem("projected")
        s_xb = sem("x_bias_done")
        s_x1 = sem("x1_done")
        s_st2 = sem("moments2_done")
        s_rs2 = sem("rstd2_done")
        s_xn2 = sem("x1_normalised")
        s_x2t = sem("xn2_turned")
        s_x2c = sem("xn2_t_copied")
        s_lo = sem("logits_made")
        s_lc = sem("logits_read")
        s_gap = sem("gap_ready")
        s_eg = sem("gap_exp_done")
        s_co = sem("combine_ready")
        s_gu = sem("gate_up_made")
        s_th = sem("tanh_done")
        s_ga = sem("gate_read")
        s_h = sem("h_chunk_done")
        s_ht = sem("h_turned")
        s_hc = sem("h_cols_copied")
        s_dn = sem("down_done")
        s_fi = sem("final_done")
        s_out = sem("stored")

        N_W = 11
        N_FFW = 5
        N_PAD = 5

        def wait(eng, s, n):
            if isinstance(n, int) and n <= 0:
                return
            eng.wait_ge(s, n)

        def hold(eng):
            eng.sem_inc(s_held, 1)

        def after(t, s, k):
            return (t, s + k) if s + k < HEADS else (t + 1, s + k - HEADS)

        class Chain:

            def __init__(self, eng, s):
                self.eng, self.s, self.base, self.k = eng, s, 0, 0

            def at(self, base):
                self.base, self.k = base, 0

            def inc(self, ins):
                self.k += 1
                ins.then_inc(self.s, 1)

            def step(self, ins, held=False):
                self.inc(ins)
                self.eng.wait_ge(self.s, self.base + self.k)
                if held:
                    hold(self.eng)

        block = stack.enter_context(nc.Block())

        @block.sync
        def _(sp):
            def load(dst, src):
                sp.dma_start(dst, src).then_inc(s_w, 16)

            def tile_in(n, u):
                wait(sp, s_xt, n - 1)
                sp.dma_start(ctx_tile[u], ctx_in[n]).then_inc(s_ctx[u], 16)

            for i in range(XPARTS):
                part = slice(i * TILES // XPARTS, (i + 1) * TILES // XPARTS)
                sp.dma_start(x_all[:, part, :], x[part].rearrange("t p c -> p t c")).then_inc(s_x[i], 16)
                if i == 0:
                    tile_in(0, 0)
                    tile_in(1, 1)
            load(w_qk[:, :, 0:C], w_q.rearrange("(m p) n -> p m n", p=P))
            load(w_qk[:, :, C:2 * C], w_kv.rearrange("(m p) n -> p m n", p=P)[:, :, 0:C])
            load(w_v[:, :, :], w_kv.rearrange("(m p) n -> p m n", p=P)[:, :, C:2 * C])
            load(b_qk[:, 0:C], b_q.partition_broadcast(P))
            load(b_qk[:, C:2 * C], b_kv[0:C].partition_broadcast(P))
            load(b_v[:, :], b_v_cols)
            load(w_o[:, :, :], w_p.rearrange("(m p) n -> p m n", p=P))
            load(b_o[:, :], b_p.partition_broadcast(P))
            load(w_r[:, :, :], w_route.rearrange("(m p) n -> p m n", p=P))
            load(gates[:, 0:1], g_xattn.partition_broadcast(P))
            load(gates[:, 1:2], g_ffn.partition_broadcast(P))
            sp.wait_ge(s_pad, N_PAD)
            for e in range(2):
                rows = slice(64 * (1 - e), 64 * (1 - e) + 64)
                for a in range(2):
                    sp.dma_start(q_cols[rows, e:HEADS:2, 1024 * a:1024 * (a + 1)],
                                 PT[0][rows, :].unsqueeze(1).broadcast_to([64, HEADS // 2, 1024])
                                 ).then_inc(s_zero, 16)
            with sp.Fori(1, TILES // 2) as i:
                for u in range(2):
                    tile_in(2 * i + u, u)
            sp.wait_ge(s_vr, 4)
            for m in range(CH):
                sp.dma_start(gu_w[:, m, 0, :], w_gate[m]).then_inc(s_ffw, 16)
                sp.dma_start(gu_w[:, m, 1, :], w_up[m]).then_inc(s_ffw, 16)
            sp.wait_ge(s_xs, 2 * HEADS * TILES)
            sp.dma_start(d_w[:, :, :], w_down.rearrange("(b p) n -> p b n", p=P)).then_inc(s_ffw, 16)
            with sp.Fori(0, TILES) as n:
                sp.wait_ge(s_fi, n + 1)
                sp.dma_start(out[n], x_all[:, n, :]).then_inc(s_out, 16)
            sp.wait_ge(s_out, 16 * TILES)

        @block.gpsimd
        def _(pool):
            chain = Chain(pool, s_pool)
            for ident in (id_f, id_h, id_b):
                chain.step(pool.memset(ident[:, :], 0.0))
                pool.affine_select(out=ident[:, :], in_=ident[:, :], compare_op=ALU.not_equal, fill=1.0, base=0,
                                   pattern=[[-1, P]], channel_multiplier=1).then_inc(s_id, 1)
            pool.memset(expo[:, :], -0.5).then_inc(s_id, 1)
            pool.iota(lanes[:, :], pattern=[[1, EXPERTS]], base=0, channel_multiplier=0,
                      allow_small_or_imprecise_dtypes=True).then_inc(s_id, 1)
            for u in range(2):
                pool.memset(q_pad[u], 0.0).then_inc(s_pad, 1)
            for u in range(2):
                pool.memset(k_pad[u], 0.0).then_inc(s_pad, 1)
            pool.memset(PT[0][:, :], 0.0).then_inc(s_pad, 1)
            pool.wait_ge(s_pad, N_PAD)
            pool.wait_ge(s_id, 5)

            for i in range(XPARTS):
                part = slice(i * TILES // XPARTS, (i + 1) * TILES // XPARTS)
                pool.wait_ge(s_stat, i + 1)
                chain.step(pool.tensor_scalar(vpe[:, part], mv[:, part, 1], LN_EPS, None, ALU.add))
                pool.tensor_tensor(rstd[:, part, 0], vpe[:, part], expo[:, part], ALU.pow).then_inc(s_rstd, 1)

            hat = k_hat.rearrange("p (h d) -> p h d", h=HEADS)
            rest = k_rest.rearrange("p (h d) -> p h d", h=HEADS)

            def split_k(n, u):
                chain.at(3 + XPARTS + POOL_A * n)
                pool.wait_ge(s_ki, n + 1)
                chain.step(pool.tensor_tensor(
                    hat, k_int[u].rearrange("p (h d) -> p h d", h=HEADS),
                    s_all[:, n, HEADS:2 * HEADS].unsqueeze(2).broadcast_to([P, HEADS, HD]), ALU.mult))
                wait(pool, s_kt, n - 1)
                hold(pool)
                chain.step(pool.tensor_copy(k_pad[u][:, :, 0, :], hat))
                chain.step(pool.tensor_tensor(rest, hat, k_pad[u][:, :, 0, :], ALU.subtract), held=True)
                chain.step(pool.tensor_copy(k_pad[u][:, :, 1, :], rest))
                pool.tensor_tensor(k_pad[u][:, :, 2, :], rest, k_pad[u][:, :, 1, :], ALU.subtract).then_inc(s_kp, 1)
                assert chain.k == POOL_A

            split_k(0, 0)
            split_k(1, 1)
            with pool.Fori(1, TILES // 2) as i:
                for u in range(2):
                    split_k(2 * i + u, u)
            end_a = 3 + XPARTS + POOL_A * TILES

            def front(n):
                wait(pool, s_x1, n)
                pool.tensor_tensor(x_bias, x_all[:, n, :], b_o[:, :], ALU.add).then_inc(s_xb, 1)
                pool.wait_ge(s_st2, n + 1)
                hold(pool)
                chain.at(end_a + n)
                chain.step(pool.tensor_scalar(vpe2, mv2[:, 1:2], LN_EPS, None, ALU.add))
                pool.tensor_tensor(rstd2, vpe2, expo[:, 0:1], ALU.pow).then_inc(s_rs2, 1)

            pool.wait_ge(s_wp, 3)
            pool.wait_ge(s_xs, 2 * HEADS * TILES)
            front(0)
            with pool.Fori(1, TILES) as n:
                front(n)

        @block.scalar
        def _(act):
            act.wait_ge(s_w, 16 * N_W)
            act.activation(tgates[:, :], gates[:, :], ACT.Tanh).then_inc(s_tg, 1)

            def copy_turned(n, u):
                act.wait_ge(s_xt, n + 1)
                wait(act, s_qkv, n - 1)
                act.activation(turned[u], X[0][:, 512 * u:512 * u + 512], ACT.Copy).then_inc(s_tc, 1)

            def store_v(n, u):
                act.wait_ge(s_qkv, n + 1)
                for m in range(CH):
                    last = act.activation(v_ch[:, m, bass.ts(n, P)], M[u][:, bass.ts(m, P)],
                                          ACT.Identity, bias=b_v[:, m:m + 1])
                last.then_inc(s_vev, 1)

            def store_q(n):
                act.wait_ge(s_qt, n + 1)
                for e in range(2):
                    rows = slice(64 * e, 64 * e + 64)
                    last = act.activation(q_cols[rows, e:HEADS:2, bass.ts(n, P)],
                                          TB[:, :].bitcast(BF16)[rows, :].rearrange("p (j n) -> p j n", j=PAIRS),
                                          ACT.Copy)
                last.then_inc(s_qe, 1)

            def stage_a(n, u, more=True):
                if more:
                    copy_turned(n + 1, 1 - u)
                store_v(n, u)
                if not isinstance(n, int) or n >= 2:
                    store_q(n - 2)

            copy_turned(0, 0)
            stage_a(0, 0)
            stage_a(1, 1)
            with act.Fori(1, TILES // 2 - 1) as i:
                for u in range(2):
                    stage_a(2 * i + u, u)
            stage_a(TILES - 2, 0)
            stage_a(TILES - 1, 1, False)
            store_q(TILES - 2)
            store_q(TILES - 1)

            def exp_half(t, s, half):
                U = HEADS * t + s
                j = 2 * s + half
                act.wait_ge(s_xs, 2 * U + half + 1)
                if half == 0:
                    act.wait_ge(s_bi, U + 1)
                    wait(act, s_tu, 2 * U - 2)
                act.activation(E[s % 2][:, :].bitcast(U8)[:, 2 * HALF * half:2 * HALF * (half + 1):2], X[half][:, :],
                               ACT.Exp, bias=bias[:, s % 4:s % 4 + 1], scale=s_all[:, t, s:s + 1],
                               accum_out=acc_all[:, t, j:j + 1]).then_inc(s_ex, 1)

            def store_second(t, s):
                U = HEADS * t + s
                act.wait_ge(s_tu, 2 * U + 2)
                wait(act, s_pv, 2 * U - 2)
                act.activation(PT[2 + s % 2][:, :], TB16, ACT.Copy, bias=-1024.0).then_inc(s_eb, 1)

            def attend(t, last):
                for s in range(HEADS):
                    exp_half(t, s, 1)
                    if s + 1 < HEADS or not last:
                        exp_half(*after(t, s, 1), 0)
                    store_second(t, s)

            act.wait_ge(s_mark, 2)
            exp_half(0, 0, 0)
            attend(0, False)
            with act.Fori(1, TILES - 1) as t:
                attend(t, False)
            attend(TILES - 1, True)

            def copy_att(n):
                act.wait_ge(s_at, n + 1)
                act.activation(att_t, TB[:, 0:C], ACT.Copy).then_inc(s_ac, 1)

            def copy_xn2(n):
                act.wait_ge(s_x2t, n + 1)
                wait(act, s_gu, CHUNKS * n)
                act.activation(xn2_t, TB[:, C:2 * C], ACT.Copy).then_inc(s_x2c, 1)

            def route(n):
                act.wait_ge(s_gap, n + 1)
                act.activation(e_gap, gap, ACT.Exp)
                act.activation(th_sh, logits[:, EXPERTS:EXPERTS + 1], ACT.Tanh, scale=0.5).then_inc(s_eg, 1)

            def tanh_chunk(n, c):
                act.wait_ge(s_gu, CHUNKS * n + c + 1)
                wait(act, s_ga, CHUNKS * n + c - 1)
                act.activation(th[c % 2], X[0][:, 512 * (c % 2):512 * (c % 2) + CHUNK], ACT.Tanh,
                               scale=0.5).then_inc(s_th, 1)

            def copy_h(n, g):
                a, b = GROUPS[g]
                rows = LAST_BLOCK if b - a == 1 else P
                act.wait_ge(s_ht, len(GROUPS) * n + g + 1)
                wait(act, s_dn, n)
                act.activation(h_cols[0:rows, a:b, :],
                               M[g % 2][0:rows, 0:P * (b - a)].rearrange(
                                   "p (b n) -> p b n", b=b - a), ACT.Copy).then_inc(s_hc, 1)

            def ffn(n, front):
                tanh_chunk(n, 0)
                tanh_chunk(n, 1)
                if front:
                    copy_att(n + 1)
                tanh_chunk(n, 2)
                copy_h(n, 0)
                tanh_chunk(n, 3)
                copy_h(n, 1)
                tanh_chunk(n, 4)
                tanh_chunk(n, 5)
                copy_h(n, 2)
                if front:
                    copy_xn2(n + 1)
                copy_h(n, 3)
                copy_h(n, 4)
                if front:
                    route(n + 1)

            copy_att(0)
            copy_xn2(0)
            route(0)
            ffn(0, True)
            with act.Fori(1, TILES - 1) as n:
                ffn(n, True)
            ffn(TILES - 1, False)

        @block.vector
        def _(dve):
            chain = Chain(dve, s_dve)
            for i in range(2):
                dve.memset(E[i][:, :], MARK).then_inc(s_mark, 1)
            dve.wait_ge(s_w, 16 * N_W)
            dve.tensor_scalar(w_qk[:, :, 0:C], w_qk[:, :, 0:C], Q_SCALE, None, ALU.mult).then_inc(s_wp, 1)
            chain.step(dve.tensor_scalar(b_qk[:, 0:C], b_qk[:, 0:C], Q_SCALE, None, ALU.mult))
            dve.wait_ge(s_tg, 1)
            dve.tensor_scalar(b_o[:, :], b_o[:, :], tgates[:, 0:1], None, ALU.mult).then_inc(s_wp, 1)
            chain.step(dve.tensor_scalar(half_tgf[:, :], tgates[:, 1:2], 0.5, None, ALU.mult))
            BASE_A = 2

            for i in range(XPARTS):
                dve.wait_ge(s_x[i], 16)
                for n in range(i * TILES // XPARTS, (i + 1) * TILES // XPARTS):
                    chain.inc(dve.bn_stats(stats[:, n, :], x_all[:, n, :]))
                dve.wait_ge(s_dve, BASE_A + n + 1)
                for n in range(i * TILES // XPARTS, (i + 1) * TILES // XPARTS):
                    last = dve.bn_aggr(mv[:, n, :], stats[:, n, :])
                last.then_inc(s_stat, 1)
            BASE_A += TILES
            dve.wait_ge(s_stat, XPARTS)

            def normalise(n, u, part=XPARTS - 1):
                dve.wait_ge(s_rstd, part + 1)
                wait(dve, s_xt, n - 1)
                dve.tensor_scalar(xn[u], x_all[:, n, :], mv[:, n, 0:1], rstd[:, n, :], ALU.subtract,
                                  ALU.mult).then_inc(s_xn, 1)

            def quantise(n, u):
                wait(dve, s_qp, n)
                dve.wait_ge(s_qkv, n + 1)
                dve.tensor_tensor(qk, X[1][:, 512 * u:512 * u + 512], b_qk[:, :], ALU.add).then_inc(s_qkb, 1)
                dve.wait_ge(s_qkb, n + 1)
                heads = qk.rearrange("p (h d) -> p h d", h=2 * HEADS)
                chain.step(dve.tensor_reduce(amax, heads, axis=AX.X, op=ALU.max,
                                             apply_absolute_value=True))
                chain.step(dve.tensor_scalar(s_all[:, n, :], amax, 1.0 / 127.0, 1e-8, ALU.mult, ALU.max))
                chain.inc(dve.tensor_scalar(nsq_all[:, n, :], s_all[:, n, 0:HEADS], -1.0, None, ALU.mult))
                chain.step(dve.reciprocal(r_step, s_all[:, n, :]))
                chain.step(dve.tensor_tensor(heads, heads, r_step.unsqueeze(2).broadcast_to(
                    [P, 2 * HEADS, HD]), ALU.mult))
                wait(dve, s_kp, n - 1)
                dve.tensor_scalar(k_int[u], qk[:, C:2 * C], ROUND, -ROUND, ALU.add, ALU.add).then_inc(s_ki, 1)
                wait(dve, s_qt, n - 1)
                dve.tensor_scalar(
                    q_pad[u][:, :, 0:3, :],
                    qk[:, 0:C].rearrange("p (h d) -> p h d", h=HEADS).unsqueeze(2).broadcast_to([P, HEADS, 3, HD]),
                    ROUND, -ROUND, ALU.add, ALU.add).then_inc(s_qp, 1)

            def store_k(n):
                dve.wait_ge(s_kt, n + 1)
                dve.tensor_copy(k_cols[:, :, bass.ts(n, P)], OB[:, :].bitcast(BF16).rearrange(
                    "p (j n) -> p j n", j=PAIRS)).then_inc(s_ke, 1)

            def v_maxima(n):
                dve.wait_ge(s_vev, n + 1)
                chain.inc(dve.tensor_reduce(v_amax_t[:, n, :], v_ch[:, :, bass.ts(n, P)], axis=AX.X, op=ALU.max,
                                            apply_absolute_value=True))

            def stage_a(n, u, more=True):
                chain.at(BASE_A + DVE_A * n)
                if more:
                    normalise(n + 2, u)
                quantise(n, u)
                v_maxima(n)
                assert chain.k == DVE_A
                if not isinstance(n, int) or n >= 2:
                    store_k(n - 2)

            normalise(0, 0, 0)
            normalise(1, 1, 0)
            stage_a(0, 0)
            stage_a(1, 1)
            with dve.Fori(1, TILES // 2 - 1) as i:
                for u in range(2):
                    stage_a(2 * i + u, u)
            stage_a(TILES - 2, 0, False)
            stage_a(TILES - 1, 1, False)
            store_k(TILES - 2)
            store_k(TILES - 1)

            def reduce_quarter(t, s, k):
                U = HEADS * t + s
                dve.wait_ge(s_ms, QUARTERS * U + k + 1)
                dve.tensor_reduce(mx[:, s % 4, k:k + 1], M[k % 2][:, :], axis=AX.X, op=ALU.max).then_inc(s_mr, 1)

            def row_max(t, s):
                U = HEADS * t + s
                dve.wait_ge(s_mr, QUARTERS * (U + 1))
                dve.tensor_reduce(nmax[:, s % 4:s % 4 + 1], mx[:, s % 4, :], axis=AX.X, op=ALU.max).then_inc(s_nm, 1)

            def make_bias(t, s):
                U = HEADS * t + s
                dve.wait_ge(s_nm, U + 1)
                dve.tensor_scalar(bias[:, s % 4:s % 4 + 1], nmax[:, s % 4:s % 4 + 1], nsq_all[:, t, s:s + 1],
                                  LN255, ALU.mult, ALU.add).then_inc(s_bi, 1)

            def store_first(t, s):
                U = HEADS * t + s
                dve.wait_ge(s_tu, 2 * U + 1)
                wait(dve, s_pv, 2 * U - 3)
                dve.tensor_scalar(PT[s % 2][:, :], TB16, -1024.0, None, ALU.add).then_inc(s_ea, 1)

            def copy_o(t):
                dve.wait_ge(s_pv, 2 * HEADS * (t + 1))
                dve.tensor_copy(o_all[:, t, :], OB[:, 0:C]).then_inc(s_oc, 1)

            def attend(t, first, last):
                for s in range(HEADS):
                    if s == 0 and not first:
                        copy_o(t - 1)
                    store_first(t, s)
                    for k in range(QUARTERS):
                        if s + 3 < HEADS or not last:
                            reduce_quarter(*after(t, s, 3), k)
                        if s + 2 < HEADS or not last:
                            if k == 0:
                                row_max(*after(t, s, 2))
                            if k == 1:
                                make_bias(*after(t, s, 2))

            for k in range(QUARTERS):
                reduce_quarter(0, 0, k)
            row_max(0, 0)
            make_bias(0, 0)
            for k in range(QUARTERS):
                reduce_quarter(0, 1, k)
            row_max(0, 1)
            make_bias(0, 1)

            chain.at(BASE_A + DVE_A * TILES)
            chain.step(dve.tensor_reduce(v_amax[:, :], v_amax_t.rearrange("p t m -> p m t"), axis=AX.X, op=ALU.max))
            chain.step(dve.tensor_scalar(v_step[:, :], v_amax[:, :], 1.0 / 127.0, 1e-8, ALU.mult, ALU.max))
            chain.step(dve.reciprocal(v_rstep[:, :], v_step[:, :]))
            for m in range(CH):
                chain.step(dve.tensor_scalar(v_ch[:, m, :], v_ch[:, m, :], v_rstep[:, m:m + 1], ROUND, ALU.mult,
                                             ALU.add))
                dve.tensor_scalar(v_ints[:, m, :], v_ch[:, m, :], -ROUND, None, ALU.add).then_inc(s_vi, 1)
            chain.step(dve.tensor_scalar(o_scale[:, :], v_step[:, :], tgates[:, 0:1], None, ALU.mult))
            for m in range(CH):
                last = dve.tensor_scalar(w_o[:, m, :], w_o[:, m, :], o_scale[:, m:m + 1], None, ALU.mult)
            last.then_inc(s_wp, 1)
            for k in range(4):
                bank = TB if k % 2 == 0 else OB
                dve.wait_ge(s_vt, k + 1)
                dve.tensor_copy(v_rows[:, 4 * k:4 * k + 4, :].rearrange("p a c -> p (a c)"),
                                bank[:, :].bitcast(BF16)).then_inc(s_vr, 1)
            for k in range(QUARTERS):
                reduce_quarter(0, 2, k)

            attend(0, True, False)
            with dve.Fori(1, TILES - 1) as t:
                attend(t, False, False)
            attend(TILES - 1, False, True)
            copy_o(TILES - 1)

            base_c = BASE_A + DVE_A * TILES + 6
            acc = acc_all[:, :, :].rearrange("p t (h e) -> p (t h) e", e=2)
            dve.wait_ge(s_ex, 2 * HEADS * TILES)
            chain.at(base_c)
            chain.step(dve.tensor_tensor(r_sum[:, :], acc[:, :, 0], acc[:, :, 1], ALU.add))
            dve.reciprocal(rinv[:, :, :].rearrange("p t h -> p (t h)"), r_sum[:, :]).then_inc(s_ri, 1)
            dve.wait_ge(s_ri, 1)
            dve.wait_ge(s_oc, TILES)
            base_c += 1

            def normalise_att(n):
                wait(dve, s_at, n)
                dve.tensor_tensor(att.rearrange("p (h d) -> p h d", h=HEADS),
                                  o_all[:, n, :].rearrange("p (h d) -> p h d", h=HEADS),
                                  rinv[:, n, :].unsqueeze(2).broadcast_to([P, HEADS, HD]),
                                  ALU.mult).then_inc(s_an, 1)

            def residual(n):
                dve.wait_ge(s_y, n + 1)
                dve.wait_ge(s_xb, n + 1)
                dve.tensor_tensor(x_all[:, n, :], OB[:, C:2 * C], x_bias, ALU.add).then_inc(s_x1, 1)
                dve.wait_ge(s_x1, n + 1)
                hold(dve)
                chain.step(dve.bn_stats(stats2, x_all[:, n, :]), held=True)
                dve.bn_aggr(mv2, stats2).then_inc(s_st2, 1)

            def normalise_x1(n):
                dve.wait_ge(s_st2, n + 1)
                dve.wait_ge(s_rs2, n + 1)
                wait(dve, s_x2t, n)
                dve.tensor_scalar(xn2, x_all[:, n, :], mv2[:, 0:1], rstd2, ALU.subtract, ALU.mult).then_inc(s_xn2, 1)

            def route(n):
                dve.wait_ge(s_lo, n + 1)
                dve.tensor_copy(logits, TB[:, 0:EXPERTS + 1]).then_inc(s_lc, 1)
                dve.wait_ge(s_lc, n + 1)
                hold(dve)
                chain.step(dve.max(top_v, logits[:, 0:EXPERTS]), held=True)
                chain.step(dve.max_index(top_i.bitcast(U32), top_v, logits[:, 0:EXPERTS]))
                chain.step(dve.tensor_copy(top_f, top_i.bitcast(U32)))
                dve.tensor_tensor(gap, top_v[:, 1:2], top_v[:, 0:1], ALU.subtract).then_inc(s_gap, 1)
                dve.wait_ge(s_eg, n + 1)
                chain.step(dve.tensor_scalar(den, e_gap, 1.0, None, ALU.add))
                chain.step(dve.reciprocal(share[:, 0:1], den))
                chain.step(dve.tensor_scalar(share[:, 1:2], e_gap, share[:, 0:1], None, ALU.mult))
                chain.step(dve.tensor_scalar(share, share, half_tgf[:, :], None, ALU.mult))
                for k in range(2):
                    chain.step(dve.tensor_scalar(pick[:, EXPERTS * k:EXPERTS * (k + 1)], lanes[:, :],
                                                 top_f[:, k:k + 1], share[:, k:k + 1], ALU.is_equal, ALU.mult))
                chain.step(dve.tensor_scalar(sig, th_sh, 0.5, 0.5, ALU.mult, ALU.add))
                chain.step(dve.tensor_tensor(comb_all[:, n, 0:EXPERTS], pick[:, 0:EXPERTS],
                                             pick[:, EXPERTS:2 * EXPERTS], ALU.add))
                dve.tensor_scalar(comb_all[:, n, EXPERTS:EXPERTS + 1], sig, half_tgf[:, :], None,
                                  ALU.mult).then_inc(s_co, 1)

            def chunk(n, c):
                G = X[0][:, 512 * (c % 2):512 * (c % 2) + CHUNK]
                Up = X[1][:, 512 * (c % 2):512 * (c % 2) + CHUNK]
                dve.wait_ge(s_th, CHUNKS * n + c + 1)
                dve.scalar_tensor_tensor(out=ga[c % 2], in0=th[c % 2], scalar=1.0, in1=G, op0=ALU.add,
                                         op1=ALU.mult).then_inc(s_ga, 1)
                dve.wait_ge(s_ga, CHUNKS * n + c + 1)
                if c == 0:
                    dve.wait_ge(s_co, n + 1)
                    wait(dve, s_ht, len(GROUPS) * n)
                for e, a, b in ([(2 * c, 0, I_MOE), (2 * c + 1, I_MOE, CHUNK)] if 2 * c < EXPERTS
                                else [(EXPERTS, 0, CHUNK)]):
                    last = dve.scalar_tensor_tensor(
                        out=h_rows[:, CHUNK * c + a:CHUNK * c + b], in0=ga[c % 2][:, a:b],
                        scalar=comb_all[:, n, e:e + 1], in1=Up[:, a:b], op0=ALU.mult, op1=ALU.mult)
                last.then_inc(s_h, 1)

            def final(n):
                dve.wait_ge(s_dn, n + 1)
                dve.tensor_tensor(x_all[:, n, :], x_all[:, n, :], OB[:, 0:C], ALU.add).then_inc(s_fi, 1)

            def ffn(n, front):
                chain.at(base_c + DVE_FRONT * (n + 1))
                chunk(n, 0)
                if front:
                    normalise_att(n + 1)
                chunk(n, 1)
                chunk(n, 2)
                if front:
                    residual(n + 1)
                chunk(n, 3)
                if front:
                    normalise_x1(n + 1)
                chunk(n, 4)
                chunk(n, 5)
                if front:
                    route(n + 1)
                    assert chain.k == DVE_FRONT, chain.k
                final(n)

            chain.at(base_c)
            normalise_att(0)
            residual(0)
            normalise_x1(0)
            route(0)
            ffn(0, True)
            with dve.Fori(1, TILES - 1) as n:
                ffn(n, True)
            ffn(TILES - 1, False)

        @block.tensor
        def _(pe):
            def turn_tile(n, u):
                pe.wait_ge(s_ctx[u], 16 * ((n - u) // 2 + 1) if isinstance(n, int) else 8 * (n - u) + 16)
                pe.wait_ge(s_xn, n + 1)
                wait(pe, s_tc, n - 1)
                for m in range(CH):
                    pe.transpose(X[0][:, 512 * u + P * m:512 * u + P * m + P], xn[u][:, bass.ts(m, P)], id_f[:, :])
                for m in range(CH):
                    last = pe.transpose(X[0][:, 512 * u + C + P * m:512 * u + C + P * m + P],
                                        ctx_tile[u][:, bass.ts(m, P)], id_f[:, :])
                last.then_inc(s_xt, 1)

            def project(n, u):
                pe.wait_ge(s_tc, n + 1)
                wait(pe, s_qkb, n - 1)
                wait(pe, s_vev, n - 1)
                for side in range(2):
                    for m in range(CH):
                        pe.matmul(X[1][:, 512 * u + C * side:512 * u + C * side + C],
                                  turned[u][:, C * side + P * m:C * side + P * m + P],
                                  w_qk[:, m, C * side:C * side + C], start=(m == 0), stop=(m == CH - 1))
                for mo in range(CH):
                    for m in range(CH):
                        last = pe.matmul(M[u][:, bass.ts(mo, P)],
                                         w_v[:, m, bass.ts(mo, P)], turned[u][:, C + P * m:C + P * m + P],
                                         start=(m == 0), stop=(m == CH - 1))
                last.then_inc(s_qkv, 1)

            def turn_pads(n, u):
                pe.wait_ge(s_qp, n + 1)
                wait(pe, s_qe, n)
                for j in range(PAIRS):
                    last = pe.transpose(TB[:, :].bitcast(BF16)[:, bass.ts(j, P)],
                                        q_pad[u][:, 2 * j:2 * j + 2, :, :].rearrange("p h r d -> p (h r d)"),
                                        id_b[:, :])
                last.then_inc(s_qt, 1)
                pe.wait_ge(s_kp, n + 1)
                wait(pe, s_ke, n)
                for j in range(PAIRS):
                    last = pe.transpose(OB[:, :].bitcast(BF16)[:, bass.ts(j, P)],
                                        k_pad[u][:, 2 * j:2 * j + 2, :, :].rearrange("p h r d -> p (h r d)"),
                                        id_b[:, :])
                last.then_inc(s_kt, 1)

            def stage_a(n, u, more=True):
                if more:
                    turn_tile(n + 1, 1 - u)
                project(n, u)
                if not isinstance(n, int) or n >= 2:
                    turn_pads(n - 2, u)

            pe.wait_ge(s_id, 5)
            pe.wait_ge(s_pad, N_PAD)
            turn_tile(0, 0)
            pe.wait_ge(s_w, 16 * N_W)
            pe.wait_ge(s_wp, 1)
            stage_a(0, 0)
            stage_a(1, 1)
            with pe.Fori(1, TILES // 2 - 1) as i:
                for u in range(2):
                    stage_a(2 * i + u, u)
            stage_a(TILES - 2, 0)
            stage_a(TILES - 1, 1, False)
            turn_pads(TILES - 2, 0)
            turn_pads(TILES - 1, 1)

            def max_scores(t, s, k):
                wait(pe, s_mr, QUARTERS * (HEADS * t + s) + k - 1)
                pe.matmul(M[k % 2][:, :], q_cols[:, s, bass.ts(t, P)], k_cols[:, s // 2, bass.ts(k, 512)],
                          start=True, stop=True).then_inc(s_ms, 1)

            def exp_scores(t, s, half):
                wait(pe, s_ex, 2 * (HEADS * t + s) + half - 1)
                for b in range(2):
                    last = pe.matmul(X[half][:, bass.ts(b, 512)], q_cols[:, s, bass.ts(t, P)],
                                     k_cols[:, s // 2, HALF * half + 512 * b:HALF * half + 512 * b + 512],
                                     start=True, stop=True)
                last.then_inc(s_xs, 1)

            def turn_ints(t, s, half):
                U = HEADS * t + s
                pe.wait_ge(s_ex, 2 * U + half + 1)
                if half == 0:
                    wait(pe, s_eb, U)
                else:
                    pe.wait_ge(s_ea, U + 1)
                for k in range(KTH):
                    kt = KTH * half + k
                    last = pe.transpose(TB16[:, bass.ts(k, P)], E[s % 2][:, :].bitcast(F16)[:, bass.ts(kt, P)],
                                        id_h[:, :])
                last.then_inc(s_tu, 1)

            def times_v(t, s, half):
                U = HEADS * t + s
                if half == 0:
                    pe.wait_ge(s_ea, U + 1)
                    if s == 0:
                        wait(pe, s_oc, t)
                else:
                    pe.wait_ge(s_eb, U + 1)
                ints = PT[2 * half + s % 2]
                for k in range(KTH):
                    kt = KTH * half + k
                    last = pe.matmul(OB[:, HD * s:HD * s + HD], ints[:, bass.ts(k, P)],
                                     v_rows[:, kt, HD * s:HD * s + HD], start=(kt == 0), stop=(kt == KT - 1))
                last.then_inc(s_pv, 1)

            def attend(t, first, last):
                for s in range(HEADS):
                    turn_ints(t, s, 0)
                    maxima = s + 3 < HEADS or not last
                    if maxima:
                        max_scores(*after(t, s, 3), 0)
                    if not (first and s == 0):
                        times_v(t if s else t - 1, (s - 1) % HEADS, 1)
                    if maxima:
                        max_scores(*after(t, s, 3), 1)
                    if s + 1 < HEADS or not last:
                        exp_scores(*after(t, s, 1), 1)
                    turn_ints(t, s, 1)
                    if maxima:
                        max_scores(*after(t, s, 3), 2)
                    times_v(t, s, 0)
                    if maxima:
                        max_scores(*after(t, s, 3), 3)
                    if s + 2 < HEADS or not last:
                        exp_scores(*after(t, s, 2), 0)

            pe.wait_ge(s_qe, TILES)
            pe.wait_ge(s_zero, 64)
            pe.wait_ge(s_ke, TILES)
            pe.wait_ge(s_qkb, TILES)
            pe.wait_ge(s_vev, TILES)
            for k in range(QUARTERS):
                max_scores(0, 0, k)
            for half in range(2):
                exp_scores(0, 0, half)
            for k in range(QUARTERS):
                max_scores(0, 1, k)
            exp_scores(0, 1, 0)
            for k in range(2):
                max_scores(0, 2, k)
            pe.wait_ge(s_vi, CH)
            for k in range(4):
                bank = TB if k % 2 == 0 else OB
                wait(pe, s_vr, k - 1)
                for i in range(4):
                    for m in range(CH):
                        last = pe.transpose(bank[:, :].bitcast(BF16)[:, C * i + P * m:C * i + P * m + P],
                                            v_ints[:, m, bass.ts(4 * k + i, P)], id_b[:, :])
                last.then_inc(s_vt, 1)
            pe.wait_ge(s_vr, 4)
            for k in range(2, QUARTERS):
                max_scores(0, 2, k)
            attend(0, True, False)
            with pe.Fori(1, TILES - 1) as t:
                attend(t, False, False)
            attend(TILES - 1, False, True)
            times_v(TILES - 1, HEADS - 1, 1)

            def turn_att(n):
                pe.wait_ge(s_an, n + 1)
                wait(pe, s_x2c, n)
                wait(pe, s_lc, n)
                for m in range(CH):
                    last = pe.transpose(TB[:, bass.ts(m, P)], att[:, bass.ts(m, P)], id_f[:, :])
                last.then_inc(s_at, 1)

            def project_att(n):
                pe.wait_ge(s_ac, n + 1)
                wait(pe, s_fi, n - 1)
                for m in range(CH):
                    last = pe.matmul(OB[:, C:2 * C], att_t[:, bass.ts(m, P)], w_o[:, m, :], start=(m == 0),
                                     stop=(m == CH - 1))
                last.then_inc(s_y, 1)

            def turn_xn2(n):
                pe.wait_ge(s_xn2, n + 1)
                for m in range(CH):
                    last = pe.transpose(TB[:, C + P * m:C + P * m + P], xn2[:, bass.ts(m, P)], id_f[:, :])
                last.then_inc(s_x2t, 1)

            def route(n):
                pe.wait_ge(s_x2c, n + 1)
                for m in range(CH):
                    last = pe.matmul(TB[:, 0:EXPERTS + 1], xn2_t[:, bass.ts(m, P)], w_r[:, m, :], start=(m == 0),
                                     stop=(m == CH - 1))
                last.then_inc(s_lo, 1)

            def gate_up(n, c):
                if c == 0:
                    pe.wait_ge(s_x2c, n + 1)
                wait(pe, s_ga, CHUNKS * n + c - 1)
                wait(pe, s_h, CHUNKS * n + c - 1)
                for side in range(2):
                    for m in range(CH):
                        last = pe.matmul(X[side][:, 512 * (c % 2):512 * (c % 2) + CHUNK],
                                         xn2_t[:, bass.ts(m, P)], gu_w[:, m, side, CHUNK * c:CHUNK * (c + 1)],
                                         start=(m == 0), stop=(m == CH - 1))
                last.then_inc(s_gu, 1)

            def turn_h(n, g):
                a, b = GROUPS[g]
                done = -(-min(P * b, FEATS) // CHUNK)
                pe.wait_ge(s_h, CHUNKS * n + done)
                wait(pe, s_hc, len(GROUPS) * n + (g - 1 if g >= 2 else 0))
                if b - a == 1:
                    hold(pe)
                for k in range(a, b):
                    w = min(P, FEATS - P * k)
                    last = pe.transpose(M[g % 2][0:w, P * (k - a):P * (k - a) + P],
                                        h_rows[:, P * k:P * k + w], id_f[:, :])
                last.then_inc(s_ht, 1)

            def down(n, g, front):
                pe.wait_ge(s_hc, len(GROUPS) * n + g + 1)
                if g == 0 and front:
                    pe.wait_ge(s_x1, n + 2)
                for k in range(*GROUPS[g]):
                    w = min(P, FEATS - P * k)
                    last = pe.matmul(OB[:, 0:C], h_cols[0:w, k, :], d_w[0:w, k, :], start=(k == 0),
                                     stop=(k == BLOCKS - 1))
                if g == len(GROUPS) - 1:
                    last.then_inc(s_dn, 1)

            def ffn(n, front):
                gate_up(n, 0)
                gate_up(n, 1)
                if front:
                    turn_att(n + 1)
                gate_up(n, 2)
                if front:
                    project_att(n + 1)
                turn_h(n, 0)
                gate_up(n, 3)
                down(n, 0, front)
                turn_h(n, 1)
                gate_up(n, 4)
                down(n, 1, front)
                gate_up(n, 5)
                turn_h(n, 2)
                if front:
                    turn_xn2(n + 1)
                down(n, 2, front)
                turn_h(n, 3)
                turn_h(n, 4)
                if front:
                    route(n + 1)
                down(n, 3, front)
                down(n, 4, front)

            pe.wait_ge(s_wp, 3)
            pe.wait_ge(s_oc, TILES)
            turn_att(0)
            project_att(0)
            turn_xn2(0)
            route(0)
            pe.wait_ge(s_ffw, 16 * N_FFW)
            ffn(0, True)
            with pe.Fori(1, TILES - 1) as n:
                ffn(n, True)
            ffn(TILES - 1, False)


def kernel(**inputs):
    import numpy as np
    import concourse.bacc as bacc
    from concourse import mybir as mb
    from concourse.bass_utils import run_bass_kernel_spmd

    a = {k: np.asarray(v) for k, v in inputs.items()}
    gu = a["L0_ffn_gate_up_proj"]
    gate = np.concatenate([gu[:, :I_MOE].reshape(-1, C), a["L0_ffn_sh_gate_w"]])
    up = np.concatenate([gu[:, I_MOE:].reshape(-1, C), a["L0_ffn_sh_up_w"]])
    down = np.concatenate([a["L0_ffn_down_proj"].transpose(0, 2, 1).reshape(-1, C), a["L0_ffn_sh_down_w"].T])
    laid = {
        "x": a["x"].reshape(TILES, P, C),
        "ctx": a["ctx_2048"].reshape(TILES, P, C),
        "g_xattn": a["g_xattn"],
        "g_ffn": a["g_ffn"],
        "w_q": a["L0_xattn_Wq"],
        "b_q": a["L0_xattn_bq"],
        "w_kv": a["L0_xattn_Wkv"],
        "b_kv": a["L0_xattn_bkv"],
        "b_v_cols": a["L0_xattn_bkv"][C:].reshape(CH, P).T,
        "w_p": a["L0_xattn_Wp"],
        "b_p": a["L0_xattn_bp"],
        "w_route": np.concatenate([a["L0_ffn_router_weight"], a["L0_ffn_shared_gate_w"]]).T,
        "w_gate": gate.T.reshape(CH, P, FEATS),
        "w_up": up.T.reshape(CH, P, FEATS),
        "w_down": np.concatenate([down, np.zeros((BLOCKS * P - FEATS, C), down.dtype)]),
    }
    nc = bacc.Bacc("TRN2", target_bir_lowering=False, num_devices=1)
    arrays, args = {}, []
    for name, v in laid.items():
        arrays[f"in_{name}"] = np.ascontiguousarray(v)
        args.append(nc.dram_tensor(f"in_{name}", v.shape, mb.dt.from_np(v.dtype), kind="ExternalInput").ap())
    out = nc.dram_tensor("out_y", (TILES, P, C), mb.dt.float32, kind="ExternalOutput").ap()
    build(nc, *args, out)
    r = run_bass_kernel_spmd(nc, [arrays], core_ids=[0])
    return r.results[0]["out_y"].reshape(a["x"].shape)
```

```python
import concourse.bass as bass
from concourse import mybir
from contextlib import ExitStack
import math

F32 = mybir.dt.float32
BF16 = mybir.dt.bfloat16
F16 = mybir.dt.float16
U16 = mybir.dt.uint16
U8 = mybir.dt.uint8
U32 = mybir.dt.uint32
ALU = mybir.AluOpType
ACT = mybir.ActivationFunctionType
AX = mybir.AxisListType

P = 128
TOKENS = 2048
TILES = TOKENS // P
C = 256
CH = C // P
HEADS = 16
HD = C // HEADS
PAIRS = HEADS // 2
HALF = TOKENS // 2
KT = TOKENS // P
KTH = KT // 2
QUARTERS = TOKENS // 512
XPARTS = 4
UNITS = TILES * HEADS
EXPERTS = 8
I_MOE = 176
I_SH = 704
FEATS = EXPERTS * I_MOE + I_SH
CHUNK = 2 * I_MOE
CHUNKS = FEATS // CHUNK
BLOCKS = -(-FEATS // P)
LAST_BLOCK = FEATS - (BLOCKS - 1) * P
GROUPS = [(g, min(g + 4, BLOCKS)) for g in range(0, BLOCKS, 4)]
ROUND = 1.5 * 2.0 ** 23
MARK = 0x6400
MARKS = 2.0 ** 73 * (1 + MARK / 2.0 ** 23)
LN_EPS = 1e-5
Q_SCALE = 1.0 / math.sqrt(HD)
LN255 = math.log(255.0)

DVE_A, POOL_A = 6, 4
DVE_FRONT = 12


def build(nc, x, ctx_in, g_xattn, g_ffn, w_q, b_q, w_kv, b_kv, b_v_cols, w_p, b_p, w_route, w_gate, w_up, w_down, out):
    stack = ExitStack()
    with stack:
        def sb(name, shape, dt):
            return stack.enter_context(nc.sbuf_tensor(name, shape, dt))

        def pb(name, shape, dt=F32):
            return stack.enter_context(nc.psum_tensor(name, shape, dt))

        def sem(name):
            return stack.enter_context(nc.semaphore(name))

        x_all = sb("x_all", [P, TILES, C], F32)
        k_cols = sb("k_cols", [P, PAIRS, TOKENS], BF16)
        q_cols = sb("q_cols", [P, HEADS, TOKENS], BF16)
        v_rows = sb("v_rows", [P, KT, C], BF16)
        o_all = sb("o_all", [P, TILES, C], F32)
        s_all = sb("s_all", [P, TILES, 2 * HEADS], F32)
        nsq_all = sb("nsq_all", [P, TILES, HEADS], F32)
        acc_all = sb("acc_all", [P, TILES, 2 * HEADS], F32)
        comb_all = sb("comb_all", [P, TILES, EXPERTS + 1], F32)
        gu_w = sb("gu_w", [P, CH, 2, FEATS], F32)
        d_w = k_cols[:, :, :].rearrange("p j n -> p (j n)").bitcast(F32)[:, 0:BLOCKS * C].rearrange(
            "p (b n) -> p b n", b=BLOCKS)

        w_qk = sb("w_qk", [P, CH, 2 * C], F32)
        w_v = sb("w_v", [P, CH, C], F32)
        w_o = sb("w_o", [P, CH, C], F32)
        w_r = sb("w_r", [P, CH, EXPERTS + 1], F32)
        b_qk = sb("b_qk", [P, 2 * C], F32)
        b_v = sb("b_v", [P, CH], F32)
        b_o = sb("b_o", [P, C], F32)
        gates = sb("gates", [P, 2], F32)
        tgates = sb("tgates", [P, 2], F32)
        half_tgf = sb("half_tgf", [P, 1], F32)
        id_f = sb("id_f", [P, P], F32)
        id_h = sb("id_h", [P, P], F16)
        id_b = sb("id_b", [P, P], BF16)
        lanes = sb("lanes", [P, EXPERTS], F32)
        expo = sb("expo", [P, TILES], F32)

        def carver(area):
            at = [0]

            def carve(n):
                at[0] += n
                return area[:, at[0] - n:at[0]]
            return carve

        carve = carver(gu_w[:, :, :, :].rearrange("p m g f -> p (m g f)"))
        ctx_tile = [carve(C) for _ in range(2)]
        xn = [carve(C) for _ in range(2)]
        turned = [carve(2 * C) for _ in range(2)]
        qk = carve(2 * C)
        k_int = [carve(C) for _ in range(2)]
        k_hat = carve(C)
        k_rest = carve(C)
        q_pad = [carve(2 * C).bitcast(BF16).rearrange("p (h r d) -> p h r d", h=HEADS, r=4) for _ in range(2)]
        k_pad = [carve(2 * C).bitcast(BF16).rearrange("p (h r d) -> p h r d", h=HEADS, r=4) for _ in range(2)]
        v_ints = carve(TOKENS).bitcast(BF16).rearrange("p (m n) -> p m n", m=CH)
        stats = carve(6 * TILES).rearrange("p (t k) -> p t k", t=TILES)
        mv = carve(2 * TILES).rearrange("p (t k) -> p t k", t=TILES)
        vpe = carve(TILES)
        rstd = carve(TILES).rearrange("p (t k) -> p t k", t=TILES)
        v_amax_t = carve(CH * TILES).rearrange("p (t m) -> p t m", t=TILES)
        amax = carve(2 * HEADS)
        r_step = carve(2 * HEADS)
        v_ch = o_all[:, :, :].rearrange("p t c -> p (t c)").rearrange("p (m n) -> p m n", m=CH)
        v_amax = sb("v_amax", [P, CH], F32)
        v_step = sb("v_step", [P, CH], F32)
        v_rstep = sb("v_rstep", [P, CH], F32)
        o_scale = sb("o_scale", [P, CH], F32)

        E = [sb(f"E{i}", [P, TOKENS], U16) for i in range(2)]
        PT = [sb(f"PT{i}", [P, HALF], BF16) for i in range(4)]
        mx = sb("mx", [P, 4, QUARTERS], F32)
        nmax = sb("nmax", [P, 4], F32)
        bias = sb("bias", [P, 4], F32)

        carve = carver(q_cols[:, :, :].rearrange("p h n -> p (h n)").bitcast(F32))
        att = carve(C)
        att_t = carve(C)
        x_bias = carve(C)
        small = carve(C)
        xn2 = carve(C)
        xn2_t = carve(C)
        carve(C)
        carve(C)
        h_rows = carve(FEATS)
        h_cols = carve(BLOCKS * P).rearrange("p (b n) -> p b n", b=BLOCKS)
        th = [carve(CHUNK) for _ in range(2)]
        ga = [carve(CHUNK) for _ in range(2)]
        carve = carver(small[:, 0:C - P // 2])
        stats2 = carve(6)
        mv2 = carve(2)
        vpe2 = carve(1)
        rstd2 = carve(1)
        logits = carve(EXPERTS + 1)
        top_v = carve(8)
        top_i = carve(8)
        top_f = carve(8)
        gap = carve(1)
        e_gap = carve(1)
        th_sh = carve(1)
        den = carve(1)
        share = carve(2)
        pick = carve(2 * EXPERTS)
        sig = carve(1)
        r_sum = sb("r_sum", [P, TILES, HEADS], F32)
        rinv = sb("rinv", [P, TILES, HEADS], F32)

        X = [pb(f"X{i}", [P, HALF]) for i in range(2)]
        M = [pb(f"M{i}", [P, 512]) for i in range(2)]
        TB = pb("TB", [P, 512])
        OB = pb("OB", [P, 512])
        TB16 = TB[:, :].bitcast(F16)

        s_ctx = [sem(f"ctx_loaded{u}") for u in range(2)]
        s_x = [sem(f"x_loaded{i}") for i in range(XPARTS)]
        s_w = sem("qkv_weights_loaded")
        s_wl = sem("later_weights_loaded")
        s_gw = sem("gate_up_weights_loaded")
        s_dw = sem("down_weights_loaded")
        s_id = sem("identities_made")
        s_pad = sem("pads_cleared")
        s_mark = sem("marks_set")
        s_zero = sem("other_heads_cleared")
        s_tg = sem("gate_tanh_done")
        s_wp = sem("weights_prepared")
        s_held = sem("waits_held")
        s_dve = sem("dve_chain")
        s_pool = sem("pool_chain")
        s_stat = sem("moments_done")
        s_rstd = sem("rstd_done")
        s_xn = sem("x_normalised")
        s_xt = sem("tile_turned")
        s_tc = sem("turned_copied")
        s_qkv = sem("qkv_projected")
        s_qkb = sem("qk_read")
        s_vev = sem("v_read")
        s_qp = sem("q_pad_filled")
        s_ki = sem("k_ints_made")
        s_kp = sem("k_pad_filled")
        s_qt = sem("q_turned")
        s_kt = sem("k_turned")
        s_qe = sem("q_cols_stored")
        s_ke = sem("k_cols_stored")
        s_vi = sem("v_ints_made")
        s_vt = sem("v_turned")
        s_vra = sem("v_rows_stored_by_scalar")
        s_vrd = sem("v_rows_stored_by_vector")
        s_ms = sem("max_scores_made")
        s_mr = sem("max_scores_reduced")
        s_nm = sem("row_max_ready")
        s_xs = sem("exp_scores_made")
        s_bi = sem("bias_ready")
        s_ex = sem("exp_done")
        s_tu = sem("ints_turned")
        s_ea = sem("first_half_stored")
        s_eb = sem("second_half_stored")
        s_pv = sem("pv_done")
        s_oc = sem("o_copied")
        s_ri = sem("rinv_done")
        s_an = sem("att_normalised")
        s_at = sem("att_turned")
        s_ac = sem("att_t_copied")
        s_y = sem("projected")
        s_xb = sem("x_bias_done")
        s_x1 = sem("x1_done")
        s_st2 = sem("moments2_done")
        s_rs2 = sem("rstd2_done")
        s_xn2 = sem("x1_normalised")
        s_x2t = sem("xn2_turned")
        s_x2c = sem("xn2_t_copied")
        s_lo = sem("logits_made")
        s_lc = sem("logits_read")
        s_gap = sem("gap_ready")
        s_eg = sem("gap_exp_done")
        s_co = sem("combine_ready")
        s_gu = sem("gate_up_made")
        s_th = sem("tanh_done")
        s_ga = sem("gate_read")
        s_h = sem("h_chunk_done")
        s_ht = sem("h_turned")
        s_hc = sem("h_cols_copied")
        s_dn = sem("down_done")
        s_fi = sem("final_done")
        s_out = sem("stored")

        N_W = 6
        N_WL = 5
        N_GW = 2 * CH
        N_PAD = 5

        def wait(eng, s, n):
            if isinstance(n, int) and n <= 0:
                return
            eng.wait_ge(s, n)

        def hold(eng):
            eng.sem_inc(s_held, 1)

        def after(t, s, k):
            return (t, s + k) if s + k < HEADS else (t + 1, s + k - HEADS)

        class Chain:

            def __init__(self, eng, s):
                self.eng, self.s, self.base, self.k = eng, s, 0, 0

            def at(self, base):
                self.base, self.k = base, 0

            def inc(self, ins):
                self.k += 1
                ins.then_inc(self.s, 1)

            def step(self, ins, held=False):
                self.inc(ins)
                self.eng.wait_ge(self.s, self.base + self.k)
                if held:
                    hold(self.eng)

        block = stack.enter_context(nc.Block())

        @block.sync
        def _(sp):
            def load(dst, src, done):
                sp.dma_start(dst, src).then_inc(done, 16)

            def tile_in(n, u):
                wait(sp, s_xt, n - 1)
                sp.dma_start(ctx_tile[u], ctx_in[n]).then_inc(s_ctx[u], 16)

            def load_x(i):
                part = slice(i * TILES // XPARTS, (i + 1) * TILES // XPARTS)
                sp.dma_start(x_all[:, part, :], x[part].rearrange("t p c -> p t c")).then_inc(s_x[i], 16)

            load_x(0)
            tile_in(0, 0)
            load(w_qk[:, :, 0:C], w_q.rearrange("(m p) n -> p m n", p=P), s_w)
            load(b_qk[:, 0:C], b_q.partition_broadcast(P), s_w)
            load_x(1)
            load(w_qk[:, :, C:2 * C], w_kv.rearrange("(m p) n -> p m n", p=P)[:, :, 0:C], s_w)
            load(w_v[:, :, :], w_kv.rearrange("(m p) n -> p m n", p=P)[:, :, C:2 * C], s_w)
            load(b_qk[:, C:2 * C], b_kv[0:C].partition_broadcast(P), s_w)
            load(b_v[:, :], b_v_cols, s_w)
            tile_in(1, 1)
            load_x(2)
            load_x(3)
            load(gates[:, 0:1], g_xattn.partition_broadcast(P), s_wl)
            load(gates[:, 1:2], g_ffn.partition_broadcast(P), s_wl)
            load(b_o[:, :], b_p.partition_broadcast(P), s_wl)
            load(w_o[:, :, :], w_p.rearrange("(m p) n -> p m n", p=P), s_wl)
            load(w_r[:, :, :], w_route.rearrange("(m p) n -> p m n", p=P), s_wl)
            for k in range(4):
                for u in range(2):
                    tile_in(2 * k + 2 + u, u)
                if k == 0:
                    sp.wait_ge(s_pad, N_PAD)
                e, a = k // 2, k % 2
                rows = slice(64 * (1 - e), 64 * (1 - e) + 64)
                sp.dma_start(q_cols[rows, e:HEADS:2, HALF * a:HALF * (a + 1)],
                             PT[0][rows, :].unsqueeze(1).broadcast_to([64, PAIRS, HALF])).then_inc(s_zero, 16)
            with sp.Fori(5, TILES // 2) as i:
                for u in range(2):
                    tile_in(2 * i + u, u)
            sp.wait_ge(s_vra, 2)
            sp.wait_ge(s_vrd, 2)
            for m in range(CH):
                sp.dma_start(gu_w[:, m, 0, :], w_gate[m]).then_inc(s_gw, 16)
                sp.dma_start(gu_w[:, m, 1, :], w_up[m]).then_inc(s_gw, 16)
            sp.wait_ge(s_xs, 2 * HEADS * TILES)
            sp.dma_start(d_w[:, :, :], w_down.rearrange("(b p) n -> p b n", p=P)).then_inc(s_dw, 16)
            with sp.Fori(0, TILES) as n:
                sp.wait_ge(s_fi, n + 1)
                sp.dma_start(out[n], x_all[:, n, :]).then_inc(s_out, 16)
            sp.wait_ge(s_out, 16 * TILES)

        @block.gpsimd
        def _(pool):
            chain = Chain(pool, s_pool)
            for ident in (id_f, id_h, id_b):
                chain.step(pool.memset(ident[:, :], 0.0))
                pool.affine_select(out=ident[:, :], in_=ident[:, :], compare_op=ALU.not_equal, fill=1.0, base=0,
                                   pattern=[[-1, P]], channel_multiplier=1).then_inc(s_id, 1)
            pool.memset(expo[:, :], -0.5).then_inc(s_id, 1)
            pool.iota(lanes[:, :], pattern=[[1, EXPERTS]], base=0, channel_multiplier=0,
                      allow_small_or_imprecise_dtypes=True).then_inc(s_id, 1)
            for u in range(2):
                pool.memset(q_pad[u], 0.0).then_inc(s_pad, 1)
            for u in range(2):
                pool.memset(k_pad[u], 0.0).then_inc(s_pad, 1)
            pool.memset(PT[0][:, :], 0.0).then_inc(s_pad, 1)
            pool.wait_ge(s_pad, N_PAD)
            pool.wait_ge(s_id, 5)

            for i in range(XPARTS):
                part = slice(i * TILES // XPARTS, (i + 1) * TILES // XPARTS)
                pool.wait_ge(s_stat, i + 1)
                chain.step(pool.tensor_scalar(vpe[:, part], mv[:, part, 1], LN_EPS, None, ALU.add))
                pool.tensor_tensor(rstd[:, part, 0], vpe[:, part], expo[:, part], ALU.pow).then_inc(s_rstd, 1)

            hat = k_hat.rearrange("p (h d) -> p h d", h=HEADS)
            rest = k_rest.rearrange("p (h d) -> p h d", h=HEADS)

            def split_k(n, u):
                chain.at(3 + XPARTS + POOL_A * n)
                pool.wait_ge(s_ki, n + 1)
                hold(pool)
                ints = k_int[u].rearrange("p (h d) -> p h d", h=HEADS)
                step = s_all[:, n, HEADS:2 * HEADS].unsqueeze(2).broadcast_to([P, HEADS, HD])
                chain.inc(pool.tensor_tensor(hat, ints, step, ALU.mult))
                wait(pool, s_kt, n - 1)
                hold(pool)
                chain.step(pool.tensor_tensor(k_pad[u][:, :, 0, :], ints, step, ALU.mult))
                chain.inc(pool.tensor_tensor(rest, hat, k_pad[u][:, :, 0, :], ALU.subtract))
                chain.step(pool.tensor_tensor(k_pad[u][:, :, 1, :], hat, k_pad[u][:, :, 0, :], ALU.subtract))
                pool.tensor_tensor(k_pad[u][:, :, 2, :], rest, k_pad[u][:, :, 1, :], ALU.subtract).then_inc(s_kp, 1)
                assert chain.k == POOL_A

            split_k(0, 0)
            split_k(1, 1)
            with pool.Fori(1, TILES // 2) as i:
                for u in range(2):
                    split_k(2 * i + u, u)
            end_a = 3 + XPARTS + POOL_A * TILES

            def front(n):
                wait(pool, s_x1, n)
                pool.tensor_tensor(x_bias, x_all[:, n, :], b_o[:, :], ALU.add).then_inc(s_xb, 1)
                pool.wait_ge(s_st2, n + 1)
                hold(pool)
                chain.at(end_a + n)
                chain.step(pool.tensor_scalar(vpe2, mv2[:, 1:2], LN_EPS, None, ALU.add))
                pool.tensor_tensor(rstd2, vpe2, expo[:, 0:1], ALU.pow).then_inc(s_rs2, 1)

            pool.wait_ge(s_wp, 4)
            pool.wait_ge(s_xs, 2 * HEADS * (TILES - 1))
            front(0)
            with pool.Fori(1, TILES) as n:
                front(n)

        @block.scalar
        def _(act):

            def copy_turned(n, u):
                wait(act, s_qkv, n - 1)
                act.wait_ge(s_xt, n + 1)
                act.activation(turned[u], X[0][:, 512 * u:512 * u + 512], ACT.Copy).then_inc(s_tc, 1)

            def store_v(n, u):
                act.wait_ge(s_qkv, n + 1)
                for m in range(CH):
                    last = act.activation(v_ch[:, m, bass.ts(n, P)], M[u][:, bass.ts(m, P)],
                                          ACT.Identity, bias=b_v[:, m:m + 1])
                last.then_inc(s_vev, 1)

            def store_q(n):
                act.wait_ge(s_qt, n + 1)
                for e in range(2):
                    rows = slice(64 * e, 64 * e + 64)
                    last = act.activation(q_cols[rows, e:HEADS:2, bass.ts(n, P)],
                                          TB[:, :].bitcast(BF16)[rows, :].rearrange("p (j n) -> p j n", j=PAIRS),
                                          ACT.Copy)
                last.then_inc(s_qe, 1)

            def store_k(n):
                act.wait_ge(s_kt, n + 1)
                act.activation(k_cols[:, :, bass.ts(n, P)], OB[:, :].bitcast(BF16).rearrange(
                    "p (j n) -> p j n", j=PAIRS), ACT.Copy).then_inc(s_ke, 1)

            def stage_a(n, u, more=True):
                if more:
                    copy_turned(n + 1, 1 - u)
                store_v(n, u)
                if not isinstance(n, int) or n >= 2:
                    store_q(n - 2)
                    store_k(n - 2)

            copy_turned(0, 0)
            act.wait_ge(s_w, 16 * N_W)
            stage_a(0, 0)
            act.wait_ge(s_wl, 16 * N_WL)
            act.activation(tgates[:, :], gates[:, :], ACT.Tanh).then_inc(s_tg, 1)
            stage_a(1, 1)
            with act.Fori(1, TILES // 2 - 1) as i:
                for u in range(2):
                    stage_a(2 * i + u, u)
            stage_a(TILES - 2, 0)
            stage_a(TILES - 1, 1, False)
            for n in range(TILES - 2, TILES):
                store_q(n)
                store_k(n)

            def exp_half(t, s, half):
                U = HEADS * t + s
                j = 2 * s + half
                if half == 0:
                    act.wait_ge(s_bi, U + 1)
                act.wait_ge(s_xs, 2 * U + half + 1)
                act.activation(E[s % 2][:, :].bitcast(U8)[:, 2 * HALF * half:2 * HALF * (half + 1):2], X[half][:, :],
                               ACT.Exp, bias=bias[:, s % 4:s % 4 + 1], scale=s_all[:, t, s:s + 1],
                               accum_out=acc_all[:, t, j:j + 1]).then_inc(s_ex, 1)

            def store_second(t, s):
                U = HEADS * t + s
                act.wait_ge(s_tu, 2 * U + 2)
                act.activation(PT[2 + s % 2][:, :], TB16, ACT.Copy, bias=-1024.0).then_inc(s_eb, 1)

            def attend(t, last):
                for s in range(HEADS):
                    exp_half(t, s, 1)
                    if s + 1 < HEADS or not last:
                        exp_half(*after(t, s, 1), 0)
                    store_second(t, s)
                    if last and s == HEADS - 3:
                        copy_att(0)

            def copy_att(n):
                act.wait_ge(s_at, n + 1)
                bank = M[0] if isinstance(n, int) and n == 0 else TB
                act.activation(att_t, bank[:, 0:C], ACT.Copy).then_inc(s_ac, 1)

            def copy_xn2(n):
                wait(act, s_gu, CHUNKS * n)
                act.wait_ge(s_x2t, n + 1)
                bank = M[0] if isinstance(n, int) and n == 0 else TB
                act.activation(xn2_t, bank[:, C:2 * C], ACT.Copy).then_inc(s_x2c, 1)

            def route(n):
                act.wait_ge(s_gap, n + 1)
                act.activation(e_gap, gap, ACT.Exp)
                act.activation(th_sh, logits[:, EXPERTS:EXPERTS + 1], ACT.Tanh, scale=0.5).then_inc(s_eg, 1)

            def tanh_chunk(n, c):
                wait(act, s_ga, CHUNKS * n + c - 1)
                act.wait_ge(s_gu, CHUNKS * n + c + 1)
                act.activation(th[c % 2], X[0][:, 512 * (c % 2):512 * (c % 2) + CHUNK], ACT.Tanh,
                               scale=0.5).then_inc(s_th, 1)

            def copy_h(n, g):
                a, b = GROUPS[g]
                rows = LAST_BLOCK if b - a == 1 else P
                wait(act, s_dn, n)
                act.wait_ge(s_ht, len(GROUPS) * n + g + 1)
                act.activation(h_cols[0:rows, a:b, :],
                               M[g % 2][0:rows, 0:P * (b - a)].rearrange(
                                   "p (b n) -> p b n", b=b - a), ACT.Copy).then_inc(s_hc, 1)

            def ffn(n, front, back=True):
                tanh_chunk(n, 0)
                if back:
                    copy_h(n - 1, 3)
                    copy_h(n - 1, 4)
                tanh_chunk(n, 1)
                if front:
                    copy_att(n + 1)
                tanh_chunk(n, 2)
                copy_h(n, 0)
                tanh_chunk(n, 3)
                copy_h(n, 1)
                tanh_chunk(n, 4)
                copy_h(n, 2)
                tanh_chunk(n, 5)
                if front:
                    copy_xn2(n + 1)
                    route(n + 1)

            def store_v_rows(i):
                k = 2 * i
                act.wait_ge(s_vt, k + 1)
                act.activation(v_rows[:, 4 * k:4 * k + 4, :].rearrange("p a c -> p (a c)"),
                               TB[:, :].bitcast(BF16), ACT.Copy).then_inc(s_vra, 1)

            act.wait_ge(s_mark, 2)
            exp_half(0, 0, 0)
            store_v_rows(0)
            store_v_rows(1)
            attend(0, False)
            with act.Fori(1, TILES - 1) as t:
                attend(t, False)
            attend(TILES - 1, True)

            copy_xn2(0)
            route(0)
            ffn(0, True, False)
            with act.Fori(1, TILES - 1) as n:
                ffn(n, True)
            ffn(TILES - 1, False)
            copy_h(TILES - 1, 3)
            copy_h(TILES - 1, 4)

        @block.vector
        def _(dve):
            chain = Chain(dve, s_dve)
            for i in range(2):
                dve.memset(E[i][:, :].bitcast(F32), MARKS).then_inc(s_mark, 1)

            def statistics(i):
                tiles = range(i * TILES // XPARTS, (i + 1) * TILES // XPARTS)
                dve.wait_ge(s_x[i], 16)
                for n in tiles:
                    chain.inc(dve.bn_stats(stats[:, n, :], x_all[:, n, :]))
                dve.wait_ge(s_dve, chain.k)
                for n in tiles:
                    last = dve.bn_aggr(mv[:, n, :], stats[:, n, :])
                last.then_inc(s_stat, 1)

            def normalise(n, u, part=XPARTS - 1):
                wait(dve, s_xt, n - 1)
                dve.wait_ge(s_rstd, part + 1)
                dve.tensor_scalar(xn[u], x_all[:, n, :], mv[:, n, 0:1], rstd[:, n, :], ALU.subtract,
                                  ALU.mult).then_inc(s_xn, 1)

            def quantise(n, u):
                wait(dve, s_qp, n)
                dve.wait_ge(s_qkv, n + 1)
                dve.tensor_tensor(qk, X[1][:, 512 * u:512 * u + 512], b_qk[:, :], ALU.add).then_inc(s_qkb, 1)
                dve.wait_ge(s_qkb, n + 1)
                heads = qk.rearrange("p (h d) -> p h d", h=2 * HEADS)
                chain.step(dve.tensor_reduce(amax, heads, axis=AX.X, op=ALU.max,
                                             apply_absolute_value=True))
                chain.step(dve.tensor_scalar(s_all[:, n, :], amax, 1.0 / 127.0, 1e-8, ALU.mult, ALU.max))
                chain.inc(dve.tensor_scalar(nsq_all[:, n, :], s_all[:, n, 0:HEADS], -1.0, None, ALU.mult))
                chain.step(dve.reciprocal(r_step, s_all[:, n, :]))
                chain.step(dve.tensor_tensor(heads, heads, r_step.unsqueeze(2).broadcast_to(
                    [P, 2 * HEADS, HD]), ALU.mult))
                wait(dve, s_kp, n - 1)
                dve.tensor_scalar(k_int[u], qk[:, C:2 * C], ROUND, -ROUND, ALU.add, ALU.add).then_inc(s_ki, 1)
                wait(dve, s_qt, n - 1)
                dve.tensor_scalar(
                    q_pad[u][:, :, 0:3, :],
                    qk[:, 0:C].rearrange("p (h d) -> p h d", h=HEADS).unsqueeze(2).broadcast_to([P, HEADS, 3, HD]),
                    ROUND, -ROUND, ALU.add, ALU.add).then_inc(s_qp, 1)

            def v_maxima(n):
                dve.wait_ge(s_vev, n + 1)
                chain.inc(dve.tensor_reduce(v_amax_t[:, n, :], v_ch[:, :, bass.ts(n, P)], axis=AX.X, op=ALU.max,
                                            apply_absolute_value=True))

            def stage_a(n, u, more=True):
                chain.at(BASE_A + DVE_A * n)
                if more:
                    normalise(n + 2, u)
                quantise(n, u)
                v_maxima(n)
                assert chain.k == DVE_A

            statistics(0)
            dve.wait_ge(s_w, 16 * N_W)
            dve.tensor_scalar(w_qk[:, :, 0:C], w_qk[:, :, 0:C], Q_SCALE, None, ALU.mult).then_inc(s_wp, 1)
            chain.step(dve.tensor_scalar(b_qk[:, 0:C], b_qk[:, 0:C], Q_SCALE, None, ALU.mult))
            dve.wait_ge(s_stat, 1)
            normalise(0, 0, 0)
            normalise(1, 1, 0)
            for i in range(1, XPARTS):
                statistics(i)
            dve.wait_ge(s_stat, XPARTS)
            BASE_A = chain.k
            stage_a(0, 0)
            stage_a(1, 1)
            with dve.Fori(1, TILES // 2 - 1) as i:
                for u in range(2):
                    stage_a(2 * i + u, u)
            stage_a(TILES - 2, 0, False)
            stage_a(TILES - 1, 1, False)

            chain.at(BASE_A + DVE_A * TILES)
            dve.wait_ge(s_dve, chain.base)
            chain.step(dve.tensor_reduce(v_amax[:, :], v_amax_t.rearrange("p t m -> p m t"), axis=AX.X, op=ALU.max))
            chain.step(dve.tensor_scalar(v_step[:, :], v_amax[:, :], 1.0 / 127.0, 1e-8, ALU.mult, ALU.max))
            chain.step(dve.reciprocal(v_rstep[:, :], v_step[:, :]))
            for m in range(CH):
                chain.step(dve.tensor_scalar(v_ch[:, m, :], v_ch[:, m, :], v_rstep[:, m:m + 1], ROUND, ALU.mult,
                                            ALU.add))
                dve.tensor_scalar(v_ints[:, m, :], v_ch[:, m, :], -ROUND, None, ALU.add).then_inc(s_vi, 1)

            def store_v(i):
                k = 2 * i + 1
                dve.wait_ge(s_vt, k + 1)
                dve.tensor_copy(v_rows[:, 4 * k:4 * k + 4, :].rearrange("p a c -> p (a c)"),
                                OB[:, :].bitcast(BF16)).then_inc(s_vrd, 1)

            def reduce_quarter(t, s, k):
                U = HEADS * t + s
                dve.wait_ge(s_ms, QUARTERS * U + k + 1)
                dve.tensor_reduce(mx[:, s % 4, k:k + 1], M[k % 2][:, :], axis=AX.X, op=ALU.max).then_inc(s_mr, 1)

            def row_max(t, s):
                U = HEADS * t + s
                dve.wait_ge(s_mr, QUARTERS * (U + 1))
                dve.tensor_reduce(nmax[:, s % 4:s % 4 + 1], mx[:, s % 4, :], axis=AX.X, op=ALU.max).then_inc(s_nm, 1)

            def make_bias(t, s):
                U = HEADS * t + s
                dve.wait_ge(s_nm, U + 1)
                dve.tensor_scalar(bias[:, s % 4:s % 4 + 1], nmax[:, s % 4:s % 4 + 1], nsq_all[:, t, s:s + 1],
                                  LN255, ALU.mult, ALU.add).then_inc(s_bi, 1)

            def store_first(t, s):
                U = HEADS * t + s
                dve.wait_ge(s_tu, 2 * U + 1)
                dve.tensor_scalar(PT[s % 2][:, :], TB16, -1024.0, None, ALU.add).then_inc(s_ea, 1)

            def copy_o(t):
                dve.wait_ge(s_pv, 2 * HEADS * (t + 1))
                dve.tensor_copy(o_all[:, t, :], OB[:, 0:C]).then_inc(s_oc, 1)

            def attend(t, first, last):
                for s in range(HEADS):
                    store_first(t, s)
                    for k in range(QUARTERS):
                        if s + 3 < HEADS or not last:
                            reduce_quarter(*after(t, s, 3), k)
                        if k == 0 and s == 0 and not first:
                            copy_o(t - 1)
                        if s + 2 < HEADS or not last:
                            if k == 0:
                                row_max(*after(t, s, 2))
                            if k == 1:
                                make_bias(*after(t, s, 2))
                    if last and s == HEADS - 4:
                        prepare_weights()
                        invert_sums(0, TILES - 1, 1)
                        dve.wait_ge(s_oc, 1)
                        normalise_att(0)
                    if last and s == HEADS - 2:
                        chain.at(base_c)
                        residual(0)
                    if last and s == HEADS - 1:
                        normalise_x1(0)

            base_c = BASE_A + DVE_A * TILES + 6
            acc = acc_all[:, :, :].rearrange("p t (h e) -> p t h e", e=2)

            def prepare_weights():
                dve.wait_ge(s_tg, 1)
                dve.tensor_scalar(b_o[:, :], b_o[:, :], tgates[:, 0:1], None, ALU.mult).then_inc(s_wp, 1)
                dve.tensor_scalar(half_tgf[:, :], tgates[:, 1:2], 0.5, None, ALU.mult).then_inc(s_wp, 1)
                chain.at(base_c - 1)
                chain.step(dve.tensor_scalar(o_scale[:, :], v_step[:, :], tgates[:, 0:1], None, ALU.mult))
                for m in range(CH):
                    last = dve.tensor_scalar(w_o[:, m, :], w_o[:, m, :], o_scale[:, m:m + 1], None, ALU.mult)
                last.then_inc(s_wp, 1)

            def invert_sums(a, b, k):
                dve.wait_ge(s_ex, 2 * HEADS * b)
                dve.tensor_tensor(r_sum[:, a:b, :], acc[:, a:b, :, 0], acc[:, a:b, :, 1], ALU.add).then_inc(s_ri, 1)
                dve.wait_ge(s_ri, k)
                dve.reciprocal(rinv[:, a:b, :], r_sum[:, a:b, :]).then_inc(s_ri, 1)
                dve.wait_ge(s_ri, k + 1)

            def normalise_att(n):
                wait(dve, s_at, n)
                dve.tensor_tensor(att.rearrange("p (h d) -> p h d", h=HEADS),
                                  o_all[:, n, :].rearrange("p (h d) -> p h d", h=HEADS),
                                  rinv[:, n, :].unsqueeze(2).broadcast_to([P, HEADS, HD]),
                                  ALU.mult).then_inc(s_an, 1)

            def residual(n):
                dve.wait_ge(s_xb, n + 1)
                dve.wait_ge(s_y, n + 1)
                bank = M[1] if isinstance(n, int) and n == 0 else OB
                dve.tensor_tensor(x_all[:, n, :], bank[:, C:2 * C], x_bias, ALU.add).then_inc(s_x1, 1)
                dve.wait_ge(s_x1, n + 1)
                hold(dve)
                chain.step(dve.bn_stats(stats2, x_all[:, n, :]), held=True)
                dve.bn_aggr(mv2, stats2).then_inc(s_st2, 1)

            def normalise_x1(n):
                dve.wait_ge(s_st2, n + 1)
                wait(dve, s_x2t, n)
                dve.wait_ge(s_rs2, n + 1)
                dve.tensor_scalar(xn2, x_all[:, n, :], mv2[:, 0:1], rstd2, ALU.subtract, ALU.mult).then_inc(s_xn2, 1)

            def route(n):
                dve.wait_ge(s_lo, n + 1)
                bank = M[1] if isinstance(n, int) and n == 0 else TB
                dve.tensor_copy(logits, bank[:, 0:EXPERTS + 1]).then_inc(s_lc, 1)
                dve.wait_ge(s_lc, n + 1)
                hold(dve)
                chain.step(dve.max(top_v, logits[:, 0:EXPERTS]), held=True)
                chain.step(dve.max_index(top_i.bitcast(U32), top_v, logits[:, 0:EXPERTS]))
                chain.step(dve.tensor_copy(top_f, top_i.bitcast(U32)))
                dve.tensor_tensor(gap, top_v[:, 1:2], top_v[:, 0:1], ALU.subtract).then_inc(s_gap, 1)
                dve.wait_ge(s_eg, n + 1)
                chain.step(dve.tensor_scalar(den, e_gap, 1.0, None, ALU.add))
                chain.step(dve.reciprocal(share[:, 0:1], den))
                chain.step(dve.tensor_scalar(share[:, 1:2], e_gap, share[:, 0:1], None, ALU.mult))
                chain.step(dve.tensor_scalar(share, share, half_tgf[:, :], None, ALU.mult))
                for k in range(2):
                    chain.step(dve.tensor_scalar(pick[:, EXPERTS * k:EXPERTS * (k + 1)], lanes[:, :],
                                                 top_f[:, k:k + 1], share[:, k:k + 1], ALU.is_equal, ALU.mult))
                chain.step(dve.tensor_scalar(sig, th_sh, 0.5, 0.5, ALU.mult, ALU.add))
                chain.step(dve.tensor_tensor(comb_all[:, n, 0:EXPERTS], pick[:, 0:EXPERTS],
                                             pick[:, EXPERTS:2 * EXPERTS], ALU.add))
                dve.tensor_scalar(comb_all[:, n, EXPERTS:EXPERTS + 1], sig, half_tgf[:, :], None,
                                  ALU.mult).then_inc(s_co, 1)

            def chunk(n, c):
                G = X[0][:, 512 * (c % 2):512 * (c % 2) + CHUNK]
                Up = X[1][:, 512 * (c % 2):512 * (c % 2) + CHUNK]
                dve.wait_ge(s_th, CHUNKS * n + c + 1)
                dve.scalar_tensor_tensor(out=ga[c % 2], in0=th[c % 2], scalar=1.0, in1=G, op0=ALU.add,
                                         op1=ALU.mult).then_inc(s_ga, 1)
                dve.wait_ge(s_ga, CHUNKS * n + c + 1)
                if c == 0:
                    dve.wait_ge(s_co, n + 1)
                    wait(dve, s_ht, len(GROUPS) * n - 2)
                if c == 4:
                    wait(dve, s_ht, len(GROUPS) * n)
                for e, a, b in ([(2 * c, 0, I_MOE), (2 * c + 1, I_MOE, CHUNK)] if 2 * c < EXPERTS
                                else [(EXPERTS, 0, CHUNK)]):
                    last = dve.scalar_tensor_tensor(
                        out=h_rows[:, CHUNK * c + a:CHUNK * c + b], in0=ga[c % 2][:, a:b],
                        scalar=comb_all[:, n, e:e + 1], in1=Up[:, a:b], op0=ALU.mult, op1=ALU.mult)
                last.then_inc(s_h, 1)

            def final(n):
                dve.wait_ge(s_dn, n + 1)
                dve.tensor_tensor(x_all[:, n, :], x_all[:, n, :], OB[:, 0:C], ALU.add).then_inc(s_fi, 1)

            def ffn(n, front, back=True):
                chain.at(base_c + DVE_FRONT * (n + 1))
                chunk(n, 0)
                if front:
                    normalise_att(n + 1)
                chunk(n, 1)
                if back:
                    final(n - 1)
                chunk(n, 2)
                if front:
                    residual(n + 1)
                chunk(n, 3)
                if front:
                    normalise_x1(n + 1)
                chunk(n, 4)
                chunk(n, 5)
                if front:
                    route(n + 1)
                    assert chain.k == DVE_FRONT, chain.k

            for k in range(QUARTERS):
                reduce_quarter(0, 0, k)
            row_max(0, 0)
            make_bias(0, 0)
            for k in range(QUARTERS):
                reduce_quarter(0, 1, k)
                if k == 1:
                    store_v(0)
                    store_v(1)
            row_max(0, 1)
            make_bias(0, 1)
            for k in range(QUARTERS):
                reduce_quarter(0, 2, k)

            attend(0, True, False)
            with dve.Fori(1, TILES - 1) as t:
                attend(t, False, False)
            attend(TILES - 1, False, True)
            copy_o(TILES - 1)

            dve.wait_ge(s_wp, 4)
            chain.at(base_c + 1)
            route(0)
            invert_sums(TILES - 1, TILES, 3)
            dve.wait_ge(s_oc, TILES)
            ffn(0, True, False)
            with dve.Fori(1, TILES - 1) as n:
                ffn(n, True)
            ffn(TILES - 1, False)
            final(TILES - 1)

        @block.tensor
        def _(pe):
            def turn_tile(n, u):
                pe.wait_ge(s_ctx[u], 16 * ((n - u) // 2 + 1) if isinstance(n, int) else 8 * (n - u) + 16)
                pe.wait_ge(s_xn, n + 1)
                wait(pe, s_tc, n - 1)
                for m in range(CH):
                    pe.transpose(X[0][:, 512 * u + P * m:512 * u + P * m + P], xn[u][:, bass.ts(m, P)], id_f[:, :])
                for m in range(CH):
                    last = pe.transpose(X[0][:, 512 * u + C + P * m:512 * u + C + P * m + P],
                                        ctx_tile[u][:, bass.ts(m, P)], id_f[:, :])
                last.then_inc(s_xt, 1)

            def project(n, u):
                wait(pe, s_qkb, n - 1)
                wait(pe, s_vev, n - 1)
                pe.wait_ge(s_tc, n + 1)
                for side in range(2):
                    for m in range(CH):
                        pe.matmul(X[1][:, 512 * u + C * side:512 * u + C * side + C],
                                  turned[u][:, C * side + P * m:C * side + P * m + P],
                                  w_qk[:, m, C * side:C * side + C], start=(m == 0), stop=(m == CH - 1))
                for mo in range(CH):
                    for m in range(CH):
                        last = pe.matmul(M[u][:, bass.ts(mo, P)],
                                         w_v[:, m, bass.ts(mo, P)], turned[u][:, C + P * m:C + P * m + P],
                                         start=(m == 0), stop=(m == CH - 1))
                last.then_inc(s_qkv, 1)

            def turn_pads(n, u):
                wait(pe, s_qe, n)
                pe.wait_ge(s_qp, n + 1)
                for j in range(PAIRS):
                    last = pe.transpose(TB[:, :].bitcast(BF16)[:, bass.ts(j, P)],
                                        q_pad[u][:, 2 * j:2 * j + 2, :, :].rearrange("p h r d -> p (h r d)"),
                                        id_b[:, :])
                last.then_inc(s_qt, 1)
                wait(pe, s_ke, n)
                pe.wait_ge(s_kp, n + 1)
                for j in range(PAIRS):
                    last = pe.transpose(OB[:, :].bitcast(BF16)[:, bass.ts(j, P)],
                                        k_pad[u][:, 2 * j:2 * j + 2, :, :].rearrange("p h r d -> p (h r d)"),
                                        id_b[:, :])
                last.then_inc(s_kt, 1)

            def stage_a(n, u, more=True):
                if more:
                    turn_tile(n + 1, 1 - u)
                project(n, u)
                if not isinstance(n, int) or n >= 2:
                    turn_pads(n - 2, u)

            pe.wait_ge(s_id, 5)
            pe.wait_ge(s_pad, N_PAD)
            turn_tile(0, 0)
            pe.wait_ge(s_w, 16 * N_W)
            pe.wait_ge(s_wp, 1)
            stage_a(0, 0)
            stage_a(1, 1)
            with pe.Fori(1, TILES // 2 - 1) as i:
                for u in range(2):
                    stage_a(2 * i + u, u)
            stage_a(TILES - 2, 0)
            stage_a(TILES - 1, 1, False)
            turn_pads(TILES - 2, 0)
            turn_pads(TILES - 1, 1)

            def max_scores(t, s, k):
                wait(pe, s_mr, QUARTERS * (HEADS * t + s) + k - 1)
                pe.matmul(M[k % 2][:, :], q_cols[:, s, bass.ts(t, P)], k_cols[:, s // 2, bass.ts(k, 512)],
                          start=True, stop=True).then_inc(s_ms, 1)

            def exp_scores(t, s, half):
                wait(pe, s_ex, 2 * (HEADS * t + s) + half - 1)
                for b in range(2):
                    last = pe.matmul(X[half][:, bass.ts(b, 512)], q_cols[:, s, bass.ts(t, P)],
                                     k_cols[:, s // 2, HALF * half + 512 * b:HALF * half + 512 * b + 512],
                                     start=True, stop=True)
                last.then_inc(s_xs, 1)

            def turn_ints(t, s, half):
                U = HEADS * t + s
                pe.wait_ge(s_ex, 2 * U + half + 1)
                if half == 0:
                    wait(pe, s_eb, U)
                else:
                    pe.wait_ge(s_ea, U + 1)
                for k in range(KTH):
                    kt = KTH * half + k
                    last = pe.transpose(TB16[:, bass.ts(k, P)], E[s % 2][:, :].bitcast(F16)[:, bass.ts(kt, P)],
                                        id_h[:, :])
                last.then_inc(s_tu, 1)

            def times_v(t, s, half):
                U = HEADS * t + s
                if half == 0:
                    pe.wait_ge(s_ea, U + 1)
                    if s == 0:
                        wait(pe, s_oc, t)
                else:
                    pe.wait_ge(s_eb, U + 1)
                ints = PT[2 * half + s % 2]
                for k in range(KTH):
                    kt = KTH * half + k
                    last = pe.matmul(OB[:, HD * s:HD * s + HD], ints[:, bass.ts(k, P)],
                                     v_rows[:, kt, HD * s:HD * s + HD], start=(kt == 0), stop=(kt == KT - 1))
                last.then_inc(s_pv, 1)

            def attend(t, first, last):
                for s in range(HEADS):
                    turn_ints(t, s, 0)
                    maxima = s + 3 < HEADS or not last
                    if maxima:
                        max_scores(*after(t, s, 3), 0)
                    if not (first and s == 0):
                        times_v(t if s else t - 1, (s - 1) % HEADS, 1)
                    if maxima:
                        max_scores(*after(t, s, 3), 1)
                    if s + 1 < HEADS or not last:
                        exp_scores(*after(t, s, 1), 1)
                    turn_ints(t, s, 1)
                    if maxima:
                        max_scores(*after(t, s, 3), 2)
                    times_v(t, s, 0)
                    if maxima:
                        max_scores(*after(t, s, 3), 3)
                    if s + 2 < HEADS or not last:
                        exp_scores(*after(t, s, 2), 0)
                    if last and s == HEADS - 3:
                        pe.wait_ge(s_mr, QUARTERS * UNITS)
                        turn_att(0)
                    if last and s == HEADS - 2:
                        pe.wait_ge(s_wp, 4)
                        project_att(0)
                    if last and s == HEADS - 1:
                        turn_xn2(0)

            def turn_att(n):
                wait(pe, s_x2c, n)
                wait(pe, s_lc, n)
                pe.wait_ge(s_an, n + 1)
                bank = M[0] if isinstance(n, int) and n == 0 else TB
                for m in range(CH):
                    last = pe.transpose(bank[:, bass.ts(m, P)], att[:, bass.ts(m, P)], id_f[:, :])
                last.then_inc(s_at, 1)

            def project_att(n):
                wait(pe, s_fi, n - 1)
                pe.wait_ge(s_ac, n + 1)
                bank = M[1] if isinstance(n, int) and n == 0 else OB
                for m in range(CH):
                    last = pe.matmul(bank[:, C:2 * C], att_t[:, bass.ts(m, P)], w_o[:, m, :], start=(m == 0),
                                     stop=(m == CH - 1))
                last.then_inc(s_y, 1)

            def turn_xn2(n):
                pe.wait_ge(s_xn2, n + 1)
                bank = M[0] if isinstance(n, int) and n == 0 else TB
                for m in range(CH):
                    last = pe.transpose(bank[:, C + P * m:C + P * m + P], xn2[:, bass.ts(m, P)], id_f[:, :])
                last.then_inc(s_x2t, 1)

            def route(n):
                pe.wait_ge(s_x2c, n + 1)
                bank = M[1] if isinstance(n, int) and n == 0 else TB
                for m in range(CH):
                    last = pe.matmul(bank[:, 0:EXPERTS + 1], xn2_t[:, bass.ts(m, P)], w_r[:, m, :], start=(m == 0),
                                     stop=(m == CH - 1))
                last.then_inc(s_lo, 1)

            def gate_up(n, c):
                if c == 0:
                    pe.wait_ge(s_x2c, n + 1)
                wait(pe, s_ga, CHUNKS * n + c - 1)
                wait(pe, s_h, CHUNKS * n + c - 1)
                for side in range(2):
                    for m in range(CH):
                        last = pe.matmul(X[side][:, 512 * (c % 2):512 * (c % 2) + CHUNK],
                                         xn2_t[:, bass.ts(m, P)], gu_w[:, m, side, CHUNK * c:CHUNK * (c + 1)],
                                         start=(m == 0), stop=(m == CH - 1))
                last.then_inc(s_gu, 1)

            def turn_h(n, g):
                a, b = GROUPS[g]
                done = -(-min(P * b, FEATS) // CHUNK)
                pe.wait_ge(s_h, CHUNKS * n + done)
                wait(pe, s_hc, len(GROUPS) * n + (g - 1 if g >= 2 else 0))
                if b - a == 1:
                    hold(pe)
                for k in range(a, b):
                    w = min(P, FEATS - P * k)
                    last = pe.transpose(M[g % 2][0:w, P * (k - a):P * (k - a) + P],
                                        h_rows[:, P * k:P * k + w], id_f[:, :])
                last.then_inc(s_ht, 1)

            def down(n, g, front):
                pe.wait_ge(s_hc, len(GROUPS) * n + g + 1)
                if g == 0 and front:
                    pe.wait_ge(s_x1, n + 2)
                elif g == 0:
                    pe.wait_ge(s_fi, n)
                if g == 0:
                    pe.wait_ge(s_dw, 16)
                for k in range(*GROUPS[g]):
                    w = min(P, FEATS - P * k)
                    last = pe.matmul(OB[:, 0:C], h_cols[0:w, k, :], d_w[0:w, k, :], start=(k == 0),
                                     stop=(k == BLOCKS - 1))
                if g == len(GROUPS) - 1:
                    last.then_inc(s_dn, 1)

            def ffn(n, front, back=True):
                gate_up(n, 0)
                if back:
                    turn_h(n - 1, 3)
                    turn_h(n - 1, 4)
                gate_up(n, 1)
                if back:
                    down(n - 1, 3, True)
                    down(n - 1, 4, True)
                if front:
                    turn_att(n + 1)
                gate_up(n, 2)
                if front:
                    project_att(n + 1)
                turn_h(n, 0)
                gate_up(n, 3)
                down(n, 0, front)
                turn_h(n, 1)
                gate_up(n, 4)
                down(n, 1, front)
                turn_h(n, 2)
                gate_up(n, 5)
                if front:
                    turn_xn2(n + 1)
                down(n, 2, front)
                if front:
                    route(n + 1)

            pe.wait_ge(s_qe, TILES)
            pe.wait_ge(s_zero, 64)
            pe.wait_ge(s_ke, TILES)
            pe.wait_ge(s_qkb, TILES)
            pe.wait_ge(s_vev, TILES)
            for k in range(QUARTERS):
                max_scores(0, 0, k)
            for half in range(2):
                exp_scores(0, 0, half)
            for k in range(2):
                max_scores(0, 1, k)
            pe.wait_ge(s_vi, CH)
            for k in range(4):
                bank = TB if k % 2 == 0 else OB
                wait(pe, s_vra if k % 2 == 0 else s_vrd, k // 2)
                for i in range(4):
                    for m in range(CH):
                        last = pe.transpose(bank[:, :].bitcast(BF16)[:, C * i + P * m:C * i + P * m + P],
                                            v_ints[:, m, bass.ts(4 * k + i, P)], id_b[:, :])
                last.then_inc(s_vt, 1)
            for k in range(2, QUARTERS):
                max_scores(0, 1, k)
            exp_scores(0, 1, 0)
            for k in range(QUARTERS):
                max_scores(0, 2, k)
            pe.wait_ge(s_vra, 2)
            pe.wait_ge(s_vrd, 2)
            attend(0, True, False)
            with pe.Fori(1, TILES - 1) as t:
                attend(t, False, False)
            attend(TILES - 1, False, True)
            times_v(TILES - 1, HEADS - 1, 1)

            route(0)
            pe.wait_ge(s_gw, 16 * N_GW)
            ffn(0, True, False)
            with pe.Fori(1, TILES - 1) as n:
                ffn(n, True)
            ffn(TILES - 1, False)
            for g in (3, 4):
                turn_h(TILES - 1, g)
            for g in (3, 4):
                down(TILES - 1, g, False)


def kernel(**inputs):
    import numpy as np
    import concourse.bacc as bacc
    from concourse import mybir as mb
    from concourse.bass_utils import run_bass_kernel_spmd

    a = {k: np.asarray(v) for k, v in inputs.items()}
    gu = a["L0_ffn_gate_up_proj"]
    gate = np.concatenate([gu[:, :I_MOE].reshape(-1, C), a["L0_ffn_sh_gate_w"]])
    up = np.concatenate([gu[:, I_MOE:].reshape(-1, C), a["L0_ffn_sh_up_w"]])
    down = np.concatenate([a["L0_ffn_down_proj"].transpose(0, 2, 1).reshape(-1, C), a["L0_ffn_sh_down_w"].T])
    laid = {
        "x": a["x"].reshape(TILES, P, C),
        "ctx": a["ctx_2048"].reshape(TILES, P, C),
        "g_xattn": a["g_xattn"],
        "g_ffn": a["g_ffn"],
        "w_q": a["L0_xattn_Wq"],
        "b_q": a["L0_xattn_bq"],
        "w_kv": a["L0_xattn_Wkv"],
        "b_kv": a["L0_xattn_bkv"],
        "b_v_cols": a["L0_xattn_bkv"][C:].reshape(CH, P).T,
        "w_p": a["L0_xattn_Wp"],
        "b_p": a["L0_xattn_bp"],
        "w_route": np.concatenate([a["L0_ffn_router_weight"], a["L0_ffn_shared_gate_w"]]).T,
        "w_gate": gate.T.reshape(CH, P, FEATS),
        "w_up": up.T.reshape(CH, P, FEATS),
        "w_down": np.concatenate([down, np.zeros((BLOCKS * P - FEATS, C), down.dtype)]),
    }
    nc = bacc.Bacc("TRN2", target_bir_lowering=False, num_devices=1)
    arrays, args = {}, []
    for name, v in laid.items():
        arrays[f"in_{name}"] = np.ascontiguousarray(v)
        args.append(nc.dram_tensor(f"in_{name}", v.shape, mb.dt.from_np(v.dtype), kind="ExternalInput").ap())
    out = nc.dram_tensor("out_y", (TILES, P, C), mb.dt.float32, kind="ExternalOutput").ap()
    build(nc, *args, out)
    r = run_bass_kernel_spmd(nc, [arrays], core_ids=[0])
    return r.results[0]["out_y"].reshape(a["x"].shape)
```
